# Optimizing a Trainium2 kernel written in Bass

```python
import numpy as np
import jax
import jax.numpy as jnp

def _softmax(x, axis=-1):
    return jax.nn.softmax(x, axis=axis)

def _gelu(x):
    return jax.nn.gelu(x, approximate=True)

def _silu(x):
    return jax.nn.silu(x)

def _sigmoid(x):
    return jax.nn.sigmoid(x)

def _layernorm(x, axis=-1, eps=1e-05):
    m = jnp.mean(x, axis=axis, keepdims=True)
    v = jnp.var(x, axis=axis, keepdims=True)
    return (x - m) / jnp.sqrt(v + eps)

def _scatter_add(tgt, idx, src, axis=0):
    return tgt.at[idx].add(src)

def _segment_sum(src, seg, n):
    return jax.ops.segment_sum(src, seg, n)
kernel_name = 'mk_xattn_ffn_d1_seqx_r4_cd7249'

def setup_inputs(seed: int=0):
    np.random.seed(seed)
    _w = jnp.asarray

    def _rec_inputs():
        import jax
        import jax.numpy as jnp
        _rk = jax.random.key(seed)
        x = 7.22e-05 + 1 * jax.random.normal(jax.random.fold_in(_rk, 1), (64, 128, 256), jnp.float32)
        _lenS = 128 - jax.random.randint(jax.random.fold_in(_rk, 7), (64,), 0, max(1, 128 // 4) + 1, jnp.int32)
        _lenS2 = 128 - jax.random.randint(jax.random.fold_in(_rk, 8), (64,), 0, max(1, 128 // 4) + 1, jnp.int32)
        _ctx_1024P = jax.random.normal(jax.random.fold_in(_rk, 11), (64, 16, 256), jnp.float32)
        _ctx_1024c = jax.random.dirichlet(jax.random.fold_in(_rk, 511), 0.3 * jnp.ones((16,), jnp.float32), (64, 128))
        _ctx_1024t = jnp.einsum('bsk,bkd->bsd', _ctx_1024c, _ctx_1024P)
        _ctx_1024t = _ctx_1024t * jax.lax.rsqrt(jnp.mean(jnp.square(_ctx_1024t)) + 1e-12) * 0.953939
        ctx_1024 = 4.13588e-05 + 0.999923 * (_ctx_1024t + 0.3 * jax.random.normal(jax.random.fold_in(_rk, 611), (64, 128, 256), jnp.float32))
        return (x, ctx_1024)
    x, ctx_1024 = _rec_inputs()

    def _L0_xattn_setup():
        import jax, jax.numpy as jnp
        import numpy as np
        D_MODEL = 256
        NUM_HEADS = 16
        D_K = D_MODEL // NUM_HEADS
        key = jax.random.key(seed)
        ks = jax.random.split(key, 11)
        B, S, D = (4, 512, D_MODEL)
        s = 1.0 / np.sqrt(D)
        return {'query': jax.random.normal(ks[0], (B, S, D), jnp.float32), 'key': jax.random.normal(ks[1], (B, S, D), jnp.float32), 'value': jax.random.normal(ks[2], (B, S, D), jnp.float32), 'Wq': jax.random.normal(ks[3], (D, D), jnp.float32) * s, 'bq': jnp.zeros((D,), jnp.float32), 'Wk': jax.random.normal(ks[4], (D, D), jnp.float32) * s, 'bk': jnp.zeros((D,), jnp.float32), 'Wv': jax.random.normal(ks[5], (D, D), jnp.float32) * s, 'bv': jnp.zeros((D,), jnp.float32), 'Wo': jax.random.normal(ks[6], (D, D), jnp.float32) * s, 'bo': jnp.zeros((D,), jnp.float32)}
    _L0_xattn_all = _L0_xattn_setup()
    _L0_xattn_in = {k: v for k, v in _L0_xattn_all.items() if k in ('Wq', 'bq', 'Wk', 'bk', 'Wv', 'bv', 'Wo', 'bo')}
    del _L0_xattn_all

    def _L0_ffn_setup():
        import jax, jax.numpy as jnp
        import numpy as np
        TOP_K = 2
        key = jax.random.key(seed)
        ks = jax.random.split(key, 5)
        B, T, D, E, F = (2, 512, 256, 8, 512)
        scale_d = 1.0 / np.sqrt(D)
        scale_f = 1.0 / np.sqrt(F)
        return {'x': jax.random.normal(ks[0], (B, T, D), jnp.float32), 'kernel_router_DE': jax.random.normal(ks[1], (D, E), jnp.float32) * scale_d, 'kernel_gating_EDF': jax.random.normal(ks[2], (E, D, F), jnp.float32) * scale_d, 'kernel_up_EDF': jax.random.normal(ks[3], (E, D, F), jnp.float32) * scale_d, 'kernel_down_EFD': jax.random.normal(ks[4], (E, F, D), jnp.float32) * scale_f}
    _L0_ffn_all = _L0_ffn_setup()
    _L0_ffn_in = {k: v for k, v in _L0_ffn_all.items() if k in ('kernel_router_DE', 'kernel_gating_EDF', 'kernel_up_EDF', 'kernel_down_EFD')}
    del _L0_ffn_all
    return {'x': x, 'ctx_1024': ctx_1024, 'L0_xattn_Wq': _L0_xattn_in['Wq'], 'L0_xattn_bq': _L0_xattn_in['bq'], 'L0_xattn_Wk': _L0_xattn_in['Wk'], 'L0_xattn_bk': _L0_xattn_in['bk'], 'L0_xattn_Wv': _L0_xattn_in['Wv'], 'L0_xattn_bv': _L0_xattn_in['bv'], 'L0_xattn_Wo': _L0_xattn_in['Wo'], 'L0_xattn_bo': _L0_xattn_in['bo'], 'L0_ffn_kernel_router_DE': _L0_ffn_in['kernel_router_DE'], 'L0_ffn_kernel_gating_EDF': _L0_ffn_in['kernel_gating_EDF'], 'L0_ffn_kernel_up_EDF': _L0_ffn_in['kernel_up_EDF'], 'L0_ffn_kernel_down_EFD': _L0_ffn_in['kernel_down_EFD']}

def reference(x, ctx_1024, L0_xattn_Wq, L0_xattn_bq, L0_xattn_Wk, L0_xattn_bk, L0_xattn_Wv, L0_xattn_bv, L0_xattn_Wo, L0_xattn_bo, L0_ffn_kernel_router_DE, L0_ffn_kernel_gating_EDF, L0_ffn_kernel_up_EDF, L0_ffn_kernel_down_EFD):
    import jax
    import jax.numpy as jnp

    def _L0_xattn_ref(query, key, value, Wq, bq, Wk, bk, Wv, bv, Wo, bo):
        import jax, jax.numpy as jnp
        import numpy as np
        D_MODEL = 256
        NUM_HEADS = 16
        D_K = D_MODEL // NUM_HEADS
        B, S, D = query.shape
        H, dk = (NUM_HEADS, D_K)
        Q = (query @ Wq + bq).reshape(B, S, H, dk).transpose(0, 2, 1, 3)
        K = (key @ Wk + bk).reshape(B, S, H, dk).transpose(0, 2, 1, 3)
        V = (value @ Wv + bv).reshape(B, S, H, dk).transpose(0, 2, 1, 3)
        scores = jnp.einsum('bhqd,bhkd->bhqk', Q, K) / np.sqrt(dk).astype(np.float32)
        attn = jax.nn.softmax(scores, axis=-1)
        out = jnp.einsum('bhqk,bhkd->bhqd', attn, V)
        out = out.transpose(0, 2, 1, 3).reshape(B, S, D)
        return out @ Wo + bo

    def _L0_ffn_ref(x, kernel_router_DE, kernel_gating_EDF, kernel_up_EDF, kernel_down_EFD):
        import jax, jax.numpy as jnp
        import numpy as np
        TOP_K = 2
        E = kernel_router_DE.shape[-1]
        x = x.astype(jnp.float32)
        router_logits_BTE = jnp.einsum('BTD,DE->BTE', x, kernel_router_DE)
        probs_BTE = jax.nn.softmax(router_logits_BTE.astype(jnp.float32), axis=-1)
        weights_BTX, indices_BTX = jax.lax.top_k(probs_BTE, TOP_K)
        norm_weights_BTX = jax.nn.softmax(weights_BTX, axis=-1)
        one_hot_BTXE = jax.nn.one_hot(indices_BTX, num_classes=E, dtype=jnp.float32)
        full_weights_BTE = jnp.sum(one_hot_BTXE * norm_weights_BTX[..., None], axis=2)
        gating_BTEF = jnp.einsum('BTD,EDF->BTEF', x, kernel_gating_EDF)
        fuse_BTEF = jax.nn.silu(gating_BTEF) * jnp.einsum('BTD,EDF->BTEF', x, kernel_up_EDF)
        down_BTED = jnp.einsum('BTEF,EFD->BTED', fuse_BTEF, kernel_down_EFD)
        out_BTD = jnp.einsum('BTED,BTE->BTD', down_BTED, full_weights_BTE)
        return out_BTD.astype(jnp.float32)
    x = x + _L0_xattn_ref(_layernorm(x, axis=-1), ctx_1024, ctx_1024, L0_xattn_Wq, L0_xattn_bq, L0_xattn_Wk, L0_xattn_bk, L0_xattn_Wv, L0_xattn_bv, L0_xattn_Wo, L0_xattn_bo)
    x = x + _L0_ffn_ref(_layernorm(x, axis=-1), L0_ffn_kernel_router_DE, L0_ffn_kernel_gating_EDF, L0_ffn_kernel_up_EDF, L0_ffn_kernel_down_EFD)
    return x

_drawn_inputs = setup_inputs


def setup_inputs(seed=0):
    import zlib

    import numpy as np

    out = dict(_drawn_inputs(seed))
    spreads = {'L0_xattn_bq': (0.0, 0.1),
     'L0_xattn_bk': (0.0, 0.1),
     'L0_xattn_bv': (0.0, 0.1),
     'L0_xattn_bo': (0.0, 0.1)}
    factors = {}
    for name, (base, spread) in spreads.items():
        noise = np.random.default_rng([zlib.crc32(name.encode()), seed]).standard_normal(out[name].shape)
        drawn = base * np.exp(spread * noise) if base else spread * noise
        out[name] = jnp.asarray(drawn.astype(out[name].dtype))
    for name, factor in factors.items():
        out[name] = (out[name] * factor).astype(out[name].dtype)
    return out
```

```python
from contextlib import ExitStack

import concourse.bass as bass
from concourse import mybir

P = 128
SEQS, TOK, D = 64, 128, 256
HEADS, DK = 16, 16
EXPERTS, F = 8, 512
GROUP = 4
GROUPS = SEQS // GROUP
DC = D // P
FC = F // P
QUADS = HEADS // 4
TOKENS = SEQS * TOK
REGION = TOKENS + P
USED_TILES = 2 * TOKENS // P + EXPERTS - 1
TILES = USED_TILES + 2
TABLE = TILES + 1
SPARE_TILES = TABLE - 2 * TOKENS // P
SPARE = EXPERTS * REGION
SORTED_ROWS = SPARE + SPARE_TILES * P
EPS = 1e-5


class Steps:

    def __init__(self, eng, sem, base=0, n=0):
        self.eng, self.sem, self.base, self.n = eng, sem, base, n

    def done(self, instruction):
        self.n += 1
        instruction.then_inc(self.sem, 1)

    def wait(self):
        self.eng.wait_ge(self.sem, self.base + self.n)

    def then(self, instruction):
        self.done(instruction)
        self.wait()


def moe_attention(nc, x, ctxT, wq, bq, wk, bk, wv, bv, wo, bo, router, gating, up, down, out):
    fp32, bf16 = mybir.dt.float32, mybir.dt.bfloat16
    u32, i32 = mybir.dt.uint32, mybir.dt.int32
    ACT, ALU, AX = mybir.ActivationFunctionType, mybir.AluOpType, mybir.AxisListType

    with ExitStack() as ctx:
        def sb(name, shape, dt=fp32):
            return ctx.enter_context(nc.sbuf_tensor(name, shape, dt))

        def sem(name):
            return ctx.enter_context(nc.semaphore(name))

        sorted_x = nc.dram_tensor("sorted_x", (SORTED_ROWS, D), fp32, kind="Internal").ap()
        tile_y = nc.dram_tensor("tile_y", (TILES * P, D), fp32, kind="Internal").ap()
        resid = nc.dram_tensor("resid", (SEQS, TOK, D), fp32, kind="Internal").ap()

        wq_sb, wk_sb, wv_sb = (sb(n, [P, DC, D]) for n in ("wq_sb", "wk_sb", "wv_sb"))
        wo_sb = sb("wo_sb", [P, DC, D])
        wr_sb = sb("wr_sb", [P, DC, EXPERTS])
        bq_sb, bk_sb = sb("bq_sb", [P, DC]), sb("bk_sb", [P, DC])
        bv_sb, bo_sb = sb("bv_sb", [P, D]), sb("bo_sb", [P, D])
        gate_sb = sb("gate_sb", [P, EXPERTS * DC * F])
        up_sb = sb("up_sb", [P, EXPERTS * DC * F])
        down_sb = sb("down_sb", [P, EXPERTS * FC * D])
        ident = sb("ident", [P, P])
        before = sb("before", [P, P], bf16)
        ones = sb("ones", [P, P], bf16)
        head_rows = sb("head_rows", [P, 8])
        minus_half = sb("minus_half", [P, GROUP])
        region_base = sb("region_base", [P, EXPERTS])
        first_rank = sb("first_rank", [P, EXPERTS])
        zeros = sb("zeros", [P, D])

        x_sb = sb("x_sb", [P, GROUP, D])
        x_bo = sb("x_bo", [P, 2, GROUP, D])
        ctxT_sb = sb("ctxT_sb", [P, DC, GROUP * TOK])
        stats = sb("stats", [P, GROUP, 6])
        mean_var = sb("mean_var", [P, GROUP, 2])
        var_eps, var_eps2, rstd, rstd2 = (sb(n, [P, GROUP]) for n in ("var_eps", "var_eps2", "rstd", "rstd2"))
        xn = sb("xn", [P, GROUP, D])
        xnT = sb("xnT", [P, DC, GROUP * TOK])
        qT = sb("qT", [P, 2, DC, GROUP * TOK])
        kT = sb("kT", [P, DC, GROUP * TOK])
        k_blocks = sb("k_blocks", [P, 2, QUADS, 4 * TOK])
        v_aug = sb("v_aug", [P, GROUP, HEADS, 32])
        row_max = sb("row_max", [P, 2, 8])
        probs = sb("probs", [P, 2, 8, TOK])
        probsT = sb("probsT", [P, 2, 4 * TOK])
        attT = sb("attT", [P, QUADS * TOK])
        inv_sum = sb("inv_sum", [P, HEADS])
        attn = sb("attn", [P, D])
        attnT = sb("attnT", [P, D])
        x1 = sb("x1", [P, GROUP, D])
        xn2 = sb("xn2", [P, GROUP, D])
        xn2T = xnT
        GE = [P, GROUP, EXPERTS]
        logits, prob, tied, rest, pick1, pick2, place, picked = (
            sb(n, GE) for n in ("logits", "prob", "tied", "rest", "pick1", "pick2", "place", "picked"))
        best, total, top1, top2, rank, gap, share = (
            sb(n, [P, GROUP]) for n in ("best", "total", "top1", "top2", "rank", "gap", "share"))
        chosen = sb("chosen", GE, bf16)
        chosen_f = sb("chosen_f", GE)
        seen = sb("seen", [P, GROUP + 1, EXPERTS])
        seen_bf = sb("seen_bf", [P, GROUP + 1, EXPERTS], bf16)
        slot_f = sb("slot_f", [P, 2 * GROUP])
        weights_now = sb("weights_now", [P, 2 * GROUP])
        slots_now = sb("slots_now", [P, 2 * GROUP], u32)
        slots_all = sb("slots_all", [P, GROUPS * 2 * GROUP])
        y_rows = sb("y_rows", [P, GROUPS * 2 * GROUP], u32)
        weights_all = sb("weights_all", [P, GROUPS * 2 * GROUP])

        lane = sb("lane", [P, 1])
        count = sb("count", [P, EXPERTS])
        pad_f = sb("pad_f", [P, EXPERTS])
        pad_rows = sb("pad_rows", [P, EXPERTS], u32)
        tile_no = sb("tile_no", [1, TABLE])
        n_tiles = sb("n_tiles", [P, EXPERTS])
        closer = sb("closer", [P, EXPERTS])
        tiles_to = sb("tiles_to", [1, EXPERTS])
        table_room = k_blocks[:].rearrange("p u q t -> p (u q t)")
        past, past_tiles = (
            table_room[0:1, i:i + TABLE * EXPERTS].rearrange("p (a b) -> p a b", b=EXPERTS) for i in (0, 2560 - 1280))
        over = table_room[:, 3072:3072 + EXPERTS * (TOKENS // P)].rearrange(
            "p (e m) -> p e m", e=EXPERTS)
        edges = table_room[:, 2560:2560 + EXPERTS * (TOKENS // P)].rearrange("p (e m) -> p e m", e=EXPERTS)
        moved, rows_f = attT[:, 0:GROUPS * 2 * GROUP], attT[:, GROUPS * 2 * GROUP:2 * GROUPS * 2 * GROUP]
        expert_f, skipped, row_f = (sb(n, [1, TABLE]) for n in ("expert_f", "skipped", "row_f"))
        row_table = sb("row_table", [1, TABLE], i32)
        expert_table = sb("expert_table", [1, TABLE], i32)

        xs = x_bo[:, :, 0, :]
        xsT = xnT[:, :, 0:DC * P]
        gated, fused = qT[:, 0], kT
        fusedT = probs[:].rearrange("p u h t -> p u (h t)")[:, :, 0:F]
        ys = xn[:, 0:2, :]
        y1 = x_bo
        y2, res = (k_blocks[:, i].rearrange("p q t -> p (q t)").rearrange("p (u s d) -> p u s d", u=2, d=D)
                   for i in range(2))
        fin = probs[:].rearrange("p u h t -> p u (h t)").rearrange("p u (s d) -> p u s d", d=D)
        gather_rows = sb("gather_rows", [P, 2, 2 * GROUP], u32)
        mix = sb("mix", [P, 2, 2 * GROUP])

        score = ctx.enter_context(nc.psum_tensor("score", [P, 4, 512], fp32))
        swap = ctx.enter_context(nc.psum_tensor("swap", [P, 512], fp32))
        att = ctx.enter_context(nc.psum_tensor("att", [P, 512], fp32))
        work = ctx.enter_context(nc.psum_tensor("work", [P, 2, 512], fp32))

        s_wkvq, s_bias, s_wo, s_experts = (sem(n) for n in ("wkvq_loaded", "bias_loaded", "wo_loaded", "experts_loaded"))
        s_x, s_ctx, s_xbo = sem("x_loaded"), sem("ctx_loaded"), sem("x_bo_ready")
        s_kb = sem("keys_placed")
        s_res, s_scat, s_pad = (sem(n) for n in ("resid_stored", "rows_written", "pads_written"))
        s_zero, s_masks, s_const = (sem(n) for n in ("zeroed", "masks_ready", "consts_ready"))
        s_ln, s_rstd, s_norm = (sem(n) for n in ("ln1_steps", "rstd_ready", "x_normed"))
        s_front, s_front_v, s_front_a = (sem(n) for n in ("front_product", "front_copied_by_vector", "front_copied_by_scalar"))
        s_score, s_max, s_shift, s_exp = (sem(n) for n in ("scores_ready", "row_max_ready", "scores_shifted", "probs_ready"))
        s_swap, s_probsT, s_att, s_attT = (sem(n) for n in ("probs_swapped", "probsT_ready", "att_product", "attT_ready"))
        s_back, s_inv, s_attn = (sem(n) for n in ("att_swapped_back", "inverse_sums_ready", "attn_normalised"))
        s_fwd, s_attnT = sem("attn_swapped"), sem("attnT_ready")
        s_proj, s_x1 = sem("projected"), sem("x1_ready")
        s_rstd2, s_norm2 = sem("rstd2_ready"), sem("x1_normed")
        s_n2T, s_n2Tv, s_n2Ta = (sem(n) for n in ("x1_swapped", "x1T_copied_by_vector", "x1T_copied_by_scalar"))
        s_logit, s_route, s_lexp, s_gexp = (sem(n) for n in ("logits_ready", "route_steps", "router_exp_ready", "gap_exp_ready"))
        s_place = sem("places_ready")
        s_count, s_table = sem("counts_ready"), sem("table_steps")
        s_xs = [sem("tile_loaded_0"), sem("tile_loaded_1")]
        s_ys = [sem("tile_stored_0"), sem("tile_stored_1")]
        s_xt, s_xtc, s_gate, s_up, s_silu, s_fuse = (sem(n) for n in (
            "tile_swapped", "tileT_ready", "gate_product", "up_product", "silu_ready", "fused_ready"))
        s_ft, s_ftc, s_down, s_y = (sem(n) for n in ("fused_swapped", "fusedT_ready", "down_product", "y_ready"))
        s_rows, s_gather = sem("gather_rows_ready"), [sem("gathered_0"), sem("gathered_1")]
        s_r = [sem("resid_loaded_0"), sem("resid_loaded_1")]
        s_mix, s_half = sem("mix_ready"), sem("first_expert_added")
        s_comb = [sem("combined_0"), sem("combined_1")]
        s_out = [sem("out_stored_0"), sem("out_stored_1")]

        LN_STEPS = 3
        ROUTE_STEPS = 39
        SHIFTED = 5
        GAP = 20
        CHOSEN = 27
        PLACES_READ = 29
        TABLE_STEPS = 23
        PADS_MADE = 3
        ROWS_MADE = TABLE_STEPS + 2 + 2 * (EXPERTS - 1)

        block = ctx.enter_context(nc.Block())

        def wait(eng, semaphore, value):
            if not isinstance(value, int) or value > 0:
                eng.wait_ge(semaphore, value)

        def run_stage_a(eng, group):
            def at(g):
                group(g, g < GROUPS, 1 <= g <= GROUPS, g >= 2, g + 1 < GROUPS, g + 2 < GROUPS)

            at(0)
            at(1)
            with eng.Fori(1, GROUPS // 2 - 1) as pair:
                for u in range(2):
                    group(pair * 2 + u, True, True, True, True, True)
            for g in range(GROUPS - 2, GROUPS + 2):
                at(g)

        @block.sync
        def _(sp):
            def load_x(g):
                sp.dma_start(x_sb[:], x[bass.ds(g * GROUP, GROUP)].rearrange("s t d -> t s d")).then_inc(s_x, 16)

            def load_ctx(g):
                sp.dma_start(ctxT_sb[:], ctxT[:, bass.ds(g * GROUP * TOK, GROUP * TOK)].rearrange(
                    "(c p) t -> p c t", p=P)).then_inc(s_ctx, 16)

            load_x(0)
            load_ctx(0)
            for w_sb, w in ((wk_sb, wk), (wv_sb, wv), (wq_sb, wq)):
                sp.dma_start(w_sb[:], w.rearrange("(c p) n -> p c n", p=P)).then_inc(s_wkvq, 16)
            for b_sb, b in ((bk_sb, bk), (bq_sb, bq)):
                sp.dma_start(b_sb[:], b.rearrange("(c p) -> p c", p=P), allow_slow_non_contiguous=True).then_inc(s_bias, 16)
            for b_sb, b in ((bv_sb, bv), (bo_sb, bo)):
                sp.dma_start(b_sb[:], b.partition_broadcast(P)).then_inc(s_bias, 16)
            sp.dma_start(wo_sb[:], wo.rearrange("(c p) n -> p c n", p=P)).then_inc(s_wo, 16)
            sp.dma_start(wr_sb[:], router.rearrange("(c p) e -> p c e", p=P)).then_inc(s_wo, 16)
            for e in range(EXPERTS):
                for w_sb, w, c in ((gate_sb, gating, DC), (up_sb, up, DC), (down_sb, down, FC)):
                    n = w_sb.shape[1] // EXPERTS
                    sp.dma_start(w_sb[:, e * n:(e + 1) * n].rearrange("p (c f) -> p c f", c=c),
                                 w[e].rearrange("(c p) f -> p c f", p=P)).then_inc(s_experts, 16)
            sp.wait_ge(s_norm, 1)
            sp.wait_ge(s_xbo, 1)
            load_x(1)

            def stage_a(g, core, prev, prev2, nxt, far):
                if nxt:
                    wait(sp, s_front, g * 8 + 8)
                    load_ctx(g + 1)
                if prev:
                    wait(sp, s_x1, g * GROUP)
                    sp.dma_start(resid[bass.ds((g - 1) * GROUP, GROUP)].rearrange("s t d -> t s d"), x1[:]).then_inc(s_res, 16)
                if far:
                    wait(sp, s_xbo, g + 2)
                    load_x(g + 2)

            run_stage_a(sp, stage_a)

            sp.wait_ge(s_table, TABLE_STEPS)
            sp.wait_ge(s_scat, SPARE_TILES * 16 + GROUPS * 2 * GROUP * 16)
            sp.wait_ge(s_pad, EXPERTS * 16)

            def row_of(t):
                return sp.value_load(row_table[0:1, bass.ds(t, 1)], min_val=0, max_val=SORTED_ROWS - P)

            def load_tile(t, u):
                sp.dma_start(xs[:, u, :], sorted_x[bass.ds(row_of(t), P), :]).then_inc(s_xs[u], 16)

            def store_tile(t, u):
                sp.dma_start(tile_y[bass.ds(t * P, P), :], ys[:, u, :]).then_inc(s_ys[u], 16)

            load_tile(0, 0)
            load_tile(1, 1)
            with sp.Fori(0, (TILES - 1) // 2) as tt:
                for u in range(2):
                    t = tt * 2 + u
                    sp.wait_ge(s_xt, t + 1)
                    load_tile(t + 2, u)
                    sp.wait_ge(s_y, t + 1)
                    store_tile(t, u)
            sp.wait_ge(s_y, TILES)
            store_tile(TILES - 1, 0)

            def load_resid(g, u):
                sp.dma_start(res[:, u], resid[bass.ds(g * GROUP, GROUP)].rearrange("s t d -> t s d")).then_inc(s_r[u], 16)

            def store_out(g, u, gg):
                sp.wait_ge(s_comb[u], gg + 1)
                sp.dma_start(out[bass.ds(g * GROUP, GROUP)].rearrange("s t d -> t s d"), fin[:, u]).then_inc(s_out[u], 16)

            sp.wait_ge(s_res, GROUPS * 16)
            for u in range(2):
                load_resid(u, u)
            with sp.Fori(0, GROUPS // 2 - 1) as gg:
                for u in range(2):
                    store_out(gg * 2 + u, u, gg)
                    load_resid(gg * 2 + u + 2, u)
            for u in range(2):
                store_out(GROUPS - 2 + u, u, GROUPS // 2 - 1)
            for u in range(2):
                sp.wait_ge(s_out[u], GROUPS // 2 * 16)

        @block.gpsimd
        def _(pool):
            nc.gpsimd.memset(head_rows[:], 1.0).then_inc(s_zero, 1)
            nc.gpsimd.memset(ident[:], 0.0).then_inc(s_zero, 1)
            nc.gpsimd.memset(before[:], 1.0).then_inc(s_zero, 1)
            nc.gpsimd.memset(v_aug[:], 0.0).then_inc(s_zero, 1)
            pool.wait_ge(s_zero, 4)
            nc.gpsimd.affine_select(out=ident[:], in_=ident[:], compare_op=ALU.not_equal, fill=1.0, base=0,
                                    pattern=[[-1, P]], channel_multiplier=1).then_inc(s_masks, 1)
            nc.gpsimd.affine_select(out=before[:], in_=before[:], compare_op=ALU.is_gt, fill=0.0, base=0,
                                    pattern=[[1, P]], channel_multiplier=-1).then_inc(s_masks, 1)
            nc.gpsimd.memset(v_aug[:, :, :, DK:DK + 1], 1.0).then_inc(s_masks, 1)
            nc.gpsimd.affine_select(out=head_rows[:], in_=head_rows[:], compare_op=ALU.is_ge, fill=0.0, base=0,
                                    pattern=[[-DK, 8]], channel_multiplier=1).then_inc(s_masks, 1)
            pool.wait_ge(s_masks, 4)
            nc.gpsimd.affine_select(out=head_rows[:], in_=head_rows[:], compare_op=ALU.is_gt, fill=0.0, base=DK,
                                    pattern=[[DK, 8]], channel_multiplier=-1).then_inc(s_masks, 1)
            nc.gpsimd.memset(minus_half[:], -0.5).then_inc(s_const, 1)
            nc.gpsimd.memset(ones[:], 1.0).then_inc(s_const, 1)
            nc.gpsimd.memset(zeros[:], 0.0).then_inc(s_const, 1)
            nc.gpsimd.memset(seen[:], 0.0).then_inc(s_const, 1)
            small = dict(allow_small_or_imprecise_dtypes=True)
            nc.gpsimd.iota(region_base[:], pattern=[[REGION, EXPERTS]], base=0, channel_multiplier=0, **small).then_inc(s_const, 1)
            nc.gpsimd.iota(first_rank[:], pattern=[[-1, EXPERTS]], base=EXPERTS, channel_multiplier=0, **small).then_inc(s_const, 1)
            nc.gpsimd.iota(lane[:], pattern=[[0, 1]], base=0, channel_multiplier=1, **small).then_inc(s_const, 1)
            nc.gpsimd.iota(tile_no[:], pattern=[[1, TABLE]], base=0, channel_multiplier=0, **small).then_inc(s_const, 1)
            pool.wait_ge(s_const, 8)
            for i in range(SPARE_TILES):
                pool.dma_start(sorted_x[SPARE + i * P:SPARE + (i + 1) * P, :], zeros[:]).then_inc(s_scat, 16)

            def place_keys(g, b):
                wait(pool, s_score, g * 16 + 4 * b - 4)
                for c in range(DC):
                    nc.gpsimd.tensor_tensor(
                        k_blocks[:, b % 2, 2 * c:2 * c + 2, :].rearrange("p q (h t) -> p (q h) t", t=TOK),
                        kT[:, c, b * TOK:(b + 1) * TOK].unsqueeze(1).broadcast_to([P, 8, TOK]),
                        head_rows[:].unsqueeze(2).broadcast_to([P, 8, TOK]), ALU.mult).then_inc(s_kb, 1)

            def root(g):
                wait(pool, s_ln, g * LN_STEPS + LN_STEPS)
                nc.gpsimd.tensor_tensor(rstd[:], var_eps[:], minus_half[:], ALU.pow).then_inc(s_rstd, 1)

            def keep_x(g, u, first):
                wait(pool, s_norm, g + 1)
                if not first:
                    wait(pool, s_x1, (g - 1) * GROUP)
                nc.gpsimd.tensor_tensor(x_bo[:, u], x_sb[:], bo_sb[:].unsqueeze(1).broadcast_to([P, GROUP, D]),
                                        ALU.add).then_inc(s_xbo, 1)

            def first_keys(g):
                wait(pool, s_front_v, g * 5 + 2)
                wait(pool, s_front_a, g * 3 + 2)
                place_keys(g, 0)
                place_keys(g, 1)

            rounds = iter([0, 1, 0, 1, 0, 1, 0, 1])

            def stage_a(g, core, prev, prev2, nxt, far):
                u = next(rounds)
                if core:
                    place_keys(g, 2)
                if nxt:
                    root(g + 1)
                if core:
                    place_keys(g, 3)
                if prev2:
                    wait(pool, s_route, (g - 2) * ROUTE_STEPS + ROUTE_STEPS)
                    pool.nop(nofuse=True)
                    for i in range(2 * GROUP):
                        pool.indirect_dma_start(
                            out=sorted_x[:, :], out_offset=bass.IndirectOffsetOnAxis(ap=slots_now[:, i:i + 1], axis=0),
                            in_=xn2[:, i % GROUP, :], in_offset=None).then_inc(s_scat, 16)
                if prev:
                    wait(pool, s_route, (g - 1) * ROUTE_STEPS + LN_STEPS)
                    nc.gpsimd.tensor_tensor(rstd2[:], var_eps2[:], minus_half[:], ALU.pow).then_inc(s_rstd2, 1)
                if nxt:
                    keep_x(g + 1, 1 - u, False)
                    first_keys(g + 1)

            pool.wait_ge(s_bias, 64)
            root(0)
            keep_x(0, 0, True)
            first_keys(0)
            run_stage_a(pool, stage_a)
            small = dict(allow_small_or_imprecise_dtypes=True)
            nc.gpsimd.iota(edges, pattern=[[0, EXPERTS], [P, TOKENS // P]], base=0, channel_multiplier=0, **small).then_inc(s_const, 1)
            pool.wait_ge(s_table, PADS_MADE)
            for e in range(EXPERTS):
                pool.indirect_dma_start(
                    out=sorted_x[:, :], out_offset=bass.IndirectOffsetOnAxis(ap=pad_rows[:, e:e + 1], axis=0),
                    in_=zeros[:], in_offset=None).then_inc(s_pad, 16)

            pool.wait_ge(s_ys[0], (TILES + 1) // 2 * 16)
            pool.wait_ge(s_ys[1], TILES // 2 * 16)
            pool.wait_ge(s_table, ROWS_MADE)
            def gather_groups(gg, first):
                for u in range(2):
                    g = gg * 2 + u
                    if not first:
                        pool.wait_ge(s_comb[u], gg)
                    nc.gpsimd.tensor_copy(gather_rows[:, u, :], y_rows[:, bass.ds(g * 2 * GROUP, 2 * GROUP)]).then_inc(s_rows, 1)
                    pool.wait_ge(s_rows, g + 1)
                    pool.nop(nofuse=True)
                    for k, y in enumerate((y1, y2)):
                        for b in range(GROUP):
                            i = k * GROUP + b
                            pool.indirect_dma_start(
                                out=y[:, u, b, :], out_offset=None, in_=tile_y[:, :],
                                in_offset=bass.IndirectOffsetOnAxis(ap=gather_rows[:, u, i:i + 1], axis=0)).then_inc(s_gather[u], 16)

            gather_groups(0, True)
            with pool.Fori(1, GROUPS // 2) as gg:
                gather_groups(gg, False)

        @block.tensor
        def _(pe):
            def product(dst, pairs):
                for i, (lhsT, rhs) in enumerate(pairs):
                    last = nc.tensor.matmul(dst, lhsT, rhs, start=(i == 0), stop=(i == len(pairs) - 1))
                return last

            banks = {"qT": iter([0, 1, 0, 1, 0, 1, 0, 1])}

            def norm_swapped(g, c):
                wait(pe, s_norm, g + 1)
                if c == 1:
                    wait(pe, s_front_v, g * 5 + 1)
                for b in range(GROUP):
                    last = nc.tensor.transpose(work[:, 0, b * P:(b + 1) * P], xn[:, b, c * P:(c + 1) * P], ident[:])
                last.then_inc(s_front, 1)

            def keys(g, m):
                wait(pe, s_ctx, g * 16 + 16)
                product(work[:, m, :], [(wk_sb[:, c, m * P:(m + 1) * P], ctxT_sb[:, c, :]) for c in range(DC)]).then_inc(s_front, 1)

            def queries(g, m):
                wait(pe, s_front_v, g * 5 + 2 + m)
                wait(pe, s_front_a, g * 3 + 1)
                product(work[:, 0, :], [(wq_sb[:, c, m * P:(m + 1) * P], xnT[:, c, :]) for c in range(DC)]).then_inc(s_front, 1)

            def values(g, m):
                for s in range(2):
                    t = (2 * m + s) * TOK
                    last = product(work[:, m, s * D:(s + 1) * D], [(ctxT_sb[:, c, t:t + TOK], wv_sb[:, c, :]) for c in range(DC)])
                last.then_inc(s_front, 1)

            def scores(g, u, k):
                b, c = k // 2, k % 2
                if k == 0:
                    wait(pe, s_front_v, g * 5 + 3)
                    wait(pe, s_front_a, g * 3 + 3)
                wait(pe, s_shift, g * 8 + k - 1)
                wait(pe, s_kb, g * 8 + k + 1)
                for q in (2 * c, 2 * c + 1):
                    nc.tensor.matmul(score[:, q, :], qT[:, u, c, b * TOK:(b + 1) * TOK], k_blocks[:, b % 2, q, :],
                                     start=True, stop=True).then_inc(s_score, 1)

            def swap_probs(g, n):
                c = n // 2 % 2
                wait(pe, s_exp, g * 8 + n // 2 + 1)
                wait(pe, s_probsT, g * 16 + n)
                for j in range(4):
                    last = nc.tensor.transpose(swap[:, j * TOK:(j + 1) * TOK], probs[:, c, 4 * (n % 2) + j, :], ident[:])
                last.then_inc(s_swap, 1)

            def attend(g, n):
                b, q = n // 4, n % 4
                wait(pe, s_probsT, g * 16 + n + 1)
                if n == 0:
                    wait(pe, s_front_v, g * 5 + 5)
                if q == 0:
                    wait(pe, s_attT, g * 4 + b)
                for j in range(4):
                    last = nc.tensor.matmul(att[32 * j:32 * j + 32, q * TOK:(q + 1) * TOK], v_aug[:, b, 4 * q + j, :],
                                            probsT[:, n % 2, j * TOK:(j + 1) * TOK], start=True, stop=True)
                last.then_inc(s_att, 1)

            def swap_back(i):
                wait(pe, s_attT, i + 1)
                wait(pe, s_attn, i)
                for q in range(QUADS):
                    last = nc.tensor.transpose(work[:, 0, q * TOK:(q + 1) * TOK], attT[:, q * TOK:(q + 1) * TOK], ident[:])
                last.then_inc(s_back, 1)

            def swap_forth(i):
                wait(pe, s_attn, i + 1)
                wait(pe, s_x1, i)
                for c in range(DC):
                    last = nc.tensor.transpose(work[:, 1, c * P:(c + 1) * P], attn[:, c * P:(c + 1) * P], ident[:])
                last.then_inc(s_fwd, 1)

            def project(i):
                wait(pe, s_attnT, i + 1)
                product(work[:, 1, 0:D], [(attnT[:, c * P:(c + 1) * P], wo_sb[:, c, :]) for c in range(DC)]).then_inc(s_proj, 1)

            def x1_swapped(g, c):
                if c == 0:
                    wait(pe, s_norm2, g + 1)
                else:
                    wait(pe, s_n2Tv, g + 1)
                for b in range(GROUP):
                    last = nc.tensor.transpose(work[:, 0, b * P:(b + 1) * P], xn2[:, b, c * P:(c + 1) * P], ident[:])
                last.then_inc(s_n2T, 1)

            def route_logits(g):
                wait(pe, s_n2Ta, g + 1)
                for b in range(GROUP):
                    last = product(work[:, 0, b * EXPERTS:(b + 1) * EXPERTS],
                                   [(xn2T[:, c, b * TOK:(b + 1) * TOK], wr_sb[:, c, :]) for c in range(DC)])
                last.then_inc(s_logit, 1)

            def places(g):
                wait(pe, s_route, g * ROUTE_STEPS + CHOSEN)
                for b in range(GROUP):
                    last = product(work[:, 1, b * EXPERTS:(b + 1) * EXPERTS],
                                   [(before[:], chosen[:, b, :]), (ones[:], seen_bf[:, b, :])])
                last.then_inc(s_place, 1)

            def stage_a(g, core, prev, prev2, nxt, far):
                u = next(banks["qT"])
                old = (g - 1) * GROUP
                for k in range(8):
                    if core and k < 6:
                        scores(g, u, k + 2)
                    elif nxt:
                        scores(g + 1, 1 - u, k - 6)
                    if k == 0 and core:
                        wait(pe, s_attn, g * GROUP - 1)
                        values(g, 0)
                        wait(pe, s_x1, g * GROUP - 2)
                        values(g, 1)
                    if k == 3 and nxt:
                        norm_swapped(g + 1, 1)
                    if k == 3 and prev2:
                        if prev:
                            wait(pe, s_attnT, g * GROUP)
                        places(g - 2)
                    if k == 4 and nxt:
                        wait(pe, s_attn, g * GROUP + 1)
                        keys(g + 1, 0)
                        wait(pe, s_x1, g * GROUP)
                        keys(g + 1, 1)
                    if k == 5 and nxt:
                        queries(g + 1, 1)
                    if k == 6 and prev:
                        wait(pe, s_attn, g * GROUP + 2 if core else g * GROUP)
                        x1_swapped(g - 1, 0)
                    if k == 7 and prev:
                        x1_swapped(g - 1, 1)
                    if core:
                        swap_probs(g, 2 * k)
                        swap_probs(g, 2 * k + 1)
                        attend(g, 2 * k)
                        attend(g, 2 * k + 1)
                    if k == 0:
                        if prev:
                            swap_forth(old + 2)
                        if prev2:
                            wait(pe, s_attn, g * GROUP - 1 if prev else SEQS)
                            route_logits(g - 2)
                    if k == 1 and prev:
                        project(old + 2)
                        if prev2:
                            wait(pe, s_route, (g - 2) * ROUTE_STEPS + SHIFTED)
                        swap_back(old + 3)
                    if k == 2:
                        if prev:
                            swap_forth(old + 3)
                        if nxt:
                            wait(pe, s_attn, g * GROUP)
                            norm_swapped(g + 1, 0)
                    if k == 3:
                        if prev:
                            if prev2:
                                wait(pe, s_route, (g - 2) * ROUTE_STEPS + PLACES_READ)
                            project(old + 3)
                        if core:
                            if nxt:
                                wait(pe, s_front_a, g * 3 + 4)
                            swap_back(g * GROUP)
                    if k == 4:
                        if core:
                            if nxt:
                                wait(pe, s_front_a, g * 3 + 5)
                            swap_forth(g * GROUP)
                        if nxt:
                            queries(g + 1, 0)
                    if k == 5 and core:
                        project(g * GROUP)
                        if nxt:
                            wait(pe, s_front_a, g * 3 + 6)
                        swap_back(g * GROUP + 1)
                    if k == 6 and core:
                        swap_forth(g * GROUP + 1)
                    if k == 7 and core:
                        project(g * GROUP + 1)
                        if prev:
                            wait(pe, s_n2Ta, g)
                        swap_back(g * GROUP + 2)

            pe.wait_ge(s_wkvq, 48)
            pe.wait_ge(s_masks, 5)
            pe.wait_ge(s_const, 8)
            pe.wait_ge(s_wo, 32)
            norm_swapped(0, 0)
            norm_swapped(0, 1)
            pe.wait_ge(s_front_a, 1)
            keys(0, 0)
            keys(0, 1)
            queries(0, 0)
            queries(0, 1)
            scores(0, 0, 0)
            scores(0, 0, 1)
            run_stage_a(pe, stage_a)
            pe.wait_ge(s_route, GROUPS * ROUTE_STEPS)
            nc.tensor.matmul(work[:, 0, 0:EXPERTS], ones[:], seen_bf[:, GROUP, :], start=True, stop=True).then_inc(s_count, 1)

            def swap_tile(t, u, tt):
                pe.wait_ge(s_xs[u], tt * 16 + 16)
                pe.wait_ge(s_xtc, t)
                for c in range(DC):
                    last = nc.tensor.transpose(swap[:, c * P:(c + 1) * P], xs[:, u, c * P:(c + 1) * P], ident[:])
                last.then_inc(s_xt, 1)

            def expert_of(t):
                return pe.value_load(expert_table[0:1, bass.ds(t, 1)], min_val=0, max_val=EXPERTS - 1)

            def gate(t, u, e):
                pe.wait_ge(s_xtc, t + 1)
                product(score[:, u, :], [(xsT[:, u, c * P:(c + 1) * P], gate_sb[:, bass.ds(e * (DC * F) + c * F, F)])
                                         for c in range(DC)]).then_inc(s_gate, 1)

            def up_(t, u, e):
                product(score[:, 2 + u, :], [(xsT[:, u, c * P:(c + 1) * P], up_sb[:, bass.ds(e * (DC * F) + c * F, F)])
                                             for c in range(DC)]).then_inc(s_up, 1)

            def swap_fused(t, u):
                pe.wait_ge(s_fuse, t + 1)
                for c in range(FC):
                    last = nc.tensor.transpose(att[:, c * P:(c + 1) * P], fused[:, u, c * P:(c + 1) * P], ident[:])
                last.then_inc(s_ft, 1)

            def down_(t, u, e):
                pe.wait_ge(s_ftc, t + 1)
                product(work[:, u, 0:D], [(fusedT[:, u, c * P:(c + 1) * P], down_sb[:, bass.ds(e * (FC * D) + c * D, D)])
                                          for c in range(FC)]).then_inc(s_down, 1)

            pe.wait_ge(s_experts, EXPERTS * 3 * 16)
            pe.wait_ge(s_table, TABLE_STEPS)
            swap_tile(0, 0, 0)
            e = expert_of(0)
            gate(0, 0, e)
            up_(0, 0, e)
            swap_tile(1, 1, 0)

            with pe.Fori(0, (TILES - 1) // 2) as tt:
                for v in range(2):
                    t = tt * 2 + v + 1
                    u = (1 + v) % 2
                    e, e_last = expert_of(t), expert_of(t - 1)
                    pe.wait_ge(s_silu, t)
                    gate(t, u, e)
                    swap_fused(t - 1, 1 - u)
                    up_(t, u, e)
                    swap_tile(t + 1, 1 - u, tt + 1)
                    down_(t - 1, 1 - u, e_last)
            e = expert_of(TILES - 1)
            swap_fused(TILES - 1, 0)
            down_(TILES - 1, 0, e)

        @block.scalar
        def _(act):
            def copy_front(g, i):
                wait(act, s_front, g * 8 + (2, 4, 6)[i])
                if i == 0:
                    nc.scalar.activation(xnT[:, 1, :], work[:, 0, :], ACT.Copy).then_inc(s_front_a, 1)
                elif i == 1:
                    wait(act, s_kb, g * 8)
                    nc.scalar.activation(kT[:, 1, :], work[:, 1, :], ACT.Identity, bias=bk_sb[:, 1:2]).then_inc(s_front_a, 1)

            def copy_queries(g, u):
                wait(act, s_front, g * 8 + 6)
                nc.scalar.activation(qT[:, u, 1, :], work[:, 0, :], ACT.Identity, bias=bq_sb[:, 1:2]).then_inc(s_front_a, 1)

            def softmax_exp(g, k):
                wait(act, s_shift, g * 8 + k + 1)
                nc.scalar.activation(probs[:, k % 2], probs[:, k % 2], ACT.Exp, scale=DK ** -0.5).then_inc(s_exp, 1)

            def copy_probsT(g, n):
                wait(act, s_swap, g * 16 + n + 1)
                wait(act, s_att, g * 16 + n - 1)
                nc.scalar.activation(probsT[:, n % 2], swap[:], ACT.Copy).then_inc(s_probsT, 1)

            def copy_attT(i):
                wait(act, s_att, i * QUADS + QUADS)
                wait(act, s_back, i)
                nc.scalar.activation(attT[:], att[:], ACT.Copy).then_inc(s_attT, 1)

            def copy_attnT(i):
                wait(act, s_fwd, i + 1)
                nc.scalar.activation(attnT[:], work[:, 1, 0:D], ACT.Copy).then_inc(s_attnT, 1)

            rounds = iter([0, 1, 0, 1, 0, 1, 0, 1])

            def stage_a(g, core, prev, prev2, nxt, far):
                u = next(rounds)
                old = (g - 1) * GROUP
                for k in range(8):
                    if core:
                        softmax_exp(g, k)
                    if k in (1, 3) and prev:
                        copy_attnT(old + 2 + k // 2)
                    if k in (5, 7) and core:
                        copy_attnT(g * GROUP + (k - 5) // 2)
                    if k == 3 and nxt:
                        copy_front(g + 1, 0)
                    if k == 4 and nxt:
                        copy_front(g + 1, 1)
                    if k == 5 and nxt:
                        copy_queries(g + 1, 1 - u)
                    if k == 7 and prev:
                        wait(act, s_n2T, (g - 1) * 2 + 2)
                        nc.scalar.activation(xn2T[:, 1, :], work[:, 0, :], ACT.Copy).then_inc(s_n2Ta, 1)
                    if core:
                        copy_probsT(g, 2 * k)
                        copy_probsT(g, 2 * k + 1)
                    if k % 2 == 1 and core:
                        copy_attT(g * GROUP + k // 2)
                    if k == 1 and prev2:
                        wait(act, s_route, (g - 2) * ROUTE_STEPS + SHIFTED)
                        nc.scalar.activation(prob[:], logits[:], ACT.Exp).then_inc(s_lexp, 1)
                    if k == 2 and prev2:
                        wait(act, s_route, (g - 2) * ROUTE_STEPS + GAP)
                        nc.scalar.activation(gap[:], gap[:], ACT.Exp).then_inc(s_gexp, 1)

            act.wait_ge(s_bias, 64)
            copy_front(0, 0)
            copy_front(0, 1)
            copy_queries(0, 0)
            run_stage_a(act, stage_a)

            def silu(t, u):
                act.wait_ge(s_gate, t + 1)
                nc.scalar.activation(gated[:, u, :], score[:, u, :], ACT.Silu).then_inc(s_silu, 1)

            def copy_fusedT(t, u):
                act.wait_ge(s_ft, t + 1)
                nc.scalar.activation(fusedT[:, u, :], att[:], ACT.Copy).then_inc(s_ftc, 1)

            silu(0, 0)
            with act.Fori(0, (TILES - 1) // 2) as tt:
                for v in range(2):
                    t, u = tt * 2 + v + 1, (1 + v) % 2
                    silu(t, u)
                    copy_fusedT(t - 1, 1 - u)
            copy_fusedT(TILES - 1, 0)

        @block.vector
        def _(dve):
            def norm_stats(steps, src, eps_out):
                for b in range(GROUP):
                    last = nc.vector.bn_stats(stats[:, b, :], src[:, b, :])
                steps.then(last)
                dve.nop(nofuse=True)
                for b in range(GROUP):
                    last = nc.vector.bn_aggr(mean_var[:, b, :], stats[:, b, :])
                steps.then(last)
                steps.then(nc.vector.tensor_scalar(eps_out[:], mean_var[:, :, 1], EPS, None, ALU.add))

            def normalise(dst, src, scale, signal):
                for b in range(GROUP):
                    last = nc.vector.tensor_scalar(dst[:, b, :], src[:, b, :], mean_var[:, b, 0:1], scale[:, b:b + 1],
                                                   ALU.subtract, ALU.mult)
                last.then_inc(signal, 1)

            def over_experts(col):
                return col[:].unsqueeze(2).broadcast_to([P, GROUP, EXPERTS])

            def over_group(row):
                return row[:].unsqueeze(1).broadcast_to([P, GROUP, EXPERTS])

            def first_best(steps, values, top, pick):
                steps.then(nc.vector.reduce_max(top[:], values[:], AX.X))
                steps.then(nc.vector.tensor_tensor(tied[:], values[:], over_experts(top), ALU.is_equal))
                steps.then(nc.vector.tensor_tensor(tied[:], tied[:], over_group(first_rank), ALU.mult))
                steps.then(nc.vector.reduce_max(rank[:], tied[:], AX.X))
                steps.then(nc.vector.tensor_tensor(pick[:], tied[:], over_experts(rank), ALU.is_equal))

            def first_norm_stats(g):
                wait(dve, s_x, g * 16 + 16)
                norm_stats(Steps(dve, s_ln, g * LN_STEPS), x_sb, var_eps)

            def first_norm(g):
                wait(dve, s_rstd, g + 1)
                normalise(xn, x_sb, rstd, s_norm)

            def copy_normed(g):
                wait(dve, s_front, g * 8 + 1)
                nc.vector.tensor_copy(xnT[:, 0, :], work[:, 0, :]).then_inc(s_front_v, 1)

            def copy_keys(g):
                wait(dve, s_front, g * 8 + 3)
                wait(dve, s_kb, g * 8)
                nc.vector.tensor_scalar(kT[:, 0, :], work[:, 0, :], bk_sb[:, 0:1], None, ALU.add).then_inc(s_front_v, 1)

            def copy_queries(g, u):
                wait(dve, s_front, g * 8 + 5)
                nc.vector.tensor_scalar(qT[:, u, 0, :], work[:, 0, :], bq_sb[:, 0:1], None, ALU.add).then_inc(s_front_v, 1)

            def copy_values(g):
                for m in range(2):
                    wait(dve, s_front, g * 8 + 7 + m)
                    for s in range(2):
                        last = nc.vector.tensor_tensor(
                            v_aug[:, 2 * m + s, :, 0:DK], work[:, m, s * D:(s + 1) * D].rearrange("p (h r) -> p h r", r=DK),
                            bv_sb[:].rearrange("p (h r) -> p h r", r=DK), ALU.add)
                    last.then_inc(s_front_v, 1)

            def shift(g, k):
                c = k % 2
                s = score[:, 2 * c:2 * c + 2, :].rearrange("p q (h t) -> p (q h) t", t=TOK)
                wait(dve, s_score, g * 16 + 2 * k + 2)
                nc.vector.reduce_max(row_max[:, c, :], s, AX.X).then_inc(s_max, 1)
                wait(dve, s_max, g * 8 + k + 1)
                wait(dve, s_swap, g * 16 + 2 * k - 2)
                nc.vector.tensor_tensor(probs[:, c], s, row_max[:, c, :].unsqueeze(2).broadcast_to([P, 8, TOK]),
                                        ALU.subtract).then_inc(s_shift, 1)

            def divide_by_sums(i):
                heads = work[:, 0, :].rearrange("p (h r) -> p h r", r=32)
                wait(dve, s_back, i + 1)
                nc.vector.reciprocal(inv_sum[:], heads[:, :, DK]).then_inc(s_inv, 1)
                wait(dve, s_inv, i + 1)
                nc.vector.tensor_tensor(attn[:].rearrange("p (h r) -> p h r", r=DK), heads[:, :, 0:DK],
                                        inv_sum[:].unsqueeze(2).broadcast_to([P, HEADS, DK]), ALU.mult).then_inc(s_attn, 1)

            def add_residual(i, b, u):
                wait(dve, s_proj, i + 1)
                nc.vector.tensor_tensor(x1[:, b, :], work[:, 1, 0:D], x_bo[:, u, b, :], ALU.add).then_inc(s_x1, 1)

            def route_shift(g):
                steps = Steps(dve, s_route, g * ROUTE_STEPS, LN_STEPS)
                wait(dve, s_logit, g + 1)
                raw = work[:, 0, 0:GROUP * EXPERTS].rearrange("p (s e) -> p s e", e=EXPERTS)
                steps.then(nc.vector.reduce_max(best[:], raw, AX.X))
                steps.done(nc.vector.tensor_tensor(logits[:], raw, over_experts(best), ALU.subtract))
                assert steps.n == SHIFTED

            def route_choose(g):
                steps = Steps(dve, s_route, g * ROUTE_STEPS, SHIFTED)
                wait(dve, s_lexp, g + 1)
                steps.then(nc.vector.reduce_sum(total[:], prob[:], AX.X))
                steps.then(nc.vector.reciprocal(share[:], total[:]))
                steps.then(nc.vector.tensor_tensor(prob[:], prob[:], over_experts(share), ALU.mult))
                first_best(steps, prob, top1, pick1)
                steps.then(nc.vector.scalar_tensor_tensor(rest[:], pick1[:], -2.0, prob[:], ALU.mult, ALU.add))
                first_best(steps, rest, top2, pick2)
                steps.done(nc.vector.tensor_tensor(gap[:], top2[:], top1[:], ALU.subtract))
                assert steps.n == GAP
                steps.done(nc.vector.tensor_tensor(chosen[:], pick1[:], pick2[:], ALU.add))
                steps.then(nc.vector.tensor_tensor(chosen_f[:], pick1[:], pick2[:], ALU.add))
                for b in range(GROUP):
                    steps.then(nc.vector.tensor_tensor(seen[:, b + 1, :], seen[:, b, :], chosen_f[:, b, :], ALU.add))
                steps.then(nc.vector.tensor_copy(seen_bf[:], seen[:]))
                assert steps.n == CHOSEN
                steps.done(nc.vector.tensor_copy(seen[:, 0, :], seen[:, GROUP, :]))
                return steps.n

            def route_place(g, n):
                steps = Steps(dve, s_route, g * ROUTE_STEPS, n)
                wait(dve, s_place, g + 1)
                steps.then(nc.vector.tensor_tensor(place[:], work[:, 1, 0:GROUP * EXPERTS].rearrange("p (s e) -> p s e", e=EXPERTS),
                                                   over_group(region_base), ALU.add))
                assert steps.n == PLACES_READ, steps.n
                for k, pick in enumerate((pick1, pick2)):
                    steps.then(nc.vector.tensor_tensor(picked[:], pick[:], place[:], ALU.mult))
                    steps.then(nc.vector.reduce_sum(slot_f[:, k * GROUP:(k + 1) * GROUP], picked[:], AX.X))
                if not isinstance(g, int) or g > 0:
                    wait(dve, s_scat, SPARE_TILES * 16 + g * 2 * GROUP * 16)
                steps.done(nc.vector.tensor_copy(slots_now[:], slot_f[:]))
                steps.done(nc.vector.tensor_copy(slots_all[:, bass.ds(g * 2 * GROUP, 2 * GROUP)], slot_f[:]))
                wait(dve, s_gexp, g + 1)
                steps.then(nc.vector.tensor_scalar(total[:], gap[:], 1.0, None, ALU.add))
                steps.then(nc.vector.reciprocal(weights_now[:, 0:GROUP], total[:]))
                steps.then(nc.vector.tensor_tensor(weights_now[:, GROUP:2 * GROUP], gap[:], weights_now[:, 0:GROUP], ALU.mult))
                steps.done(nc.vector.tensor_copy(weights_all[:, bass.ds(g * 2 * GROUP, 2 * GROUP)], weights_now[:]))
                assert steps.n == ROUTE_STEPS, steps.n

            rounds = iter([0, 1, 0, 1, 0, 1, 0, 1])

            def stage_a(g, core, prev, prev2, nxt, far):
                u = next(rounds)
                old = (g - 1) * GROUP
                for k in range(8):
                    if core:
                        shift(g, k)
                    if k in (0, 2, 4) and prev:
                        b = k // 2 + 1
                        add_residual(old + b, b, 1 - u)
                        if b < 3:
                            divide_by_sums(old + b + 1)
                    if k == 4 and core:
                        divide_by_sums(g * GROUP)
                    if k == 6 and core:
                        if prev:
                            wait(dve, s_res, g * 16)
                        add_residual(g * GROUP, 0, u)
                        divide_by_sums(g * GROUP + 1)
                    if k == 0 and core:
                        copy_values(g)
                    if k == 1 and nxt:
                        first_norm_stats(g + 1)
                    if k == 1 and prev2:
                        route_shift(g - 2)
                    if k == 2 and nxt:
                        first_norm(g + 1)
                    if k == 2 and prev2:
                        chosen_at = route_choose(g - 2)
                    if k == 3 and nxt:
                        copy_normed(g + 1)
                    if k == 3 and prev2:
                        route_place(g - 2, chosen_at)
                    if k == 4 and nxt:
                        copy_keys(g + 1)
                    if k == 4 and prev:
                        wait(dve, s_x1, g * GROUP)
                        norm_stats(Steps(dve, s_route, (g - 1) * ROUTE_STEPS), x1, var_eps2)
                    if k == 5 and nxt:
                        copy_queries(g + 1, 1 - u)
                    if k == 5 and prev:
                        wait(dve, s_rstd2, g)
                        wait(dve, s_scat, SPARE_TILES * 16 + (g - 1) * 2 * GROUP * 16)
                        normalise(xn2, x1, rstd2, s_norm2)
                    if k == 6 and prev:
                        wait(dve, s_n2T, (g - 1) * 2 + 1)
                        nc.vector.tensor_copy(xn2T[:, 0, :], work[:, 0, :]).then_inc(s_n2Tv, 1)

            dve.wait_ge(s_bias, 64)
            dve.wait_ge(s_const, 8)
            dve.wait_ge(s_masks, 5)
            first_norm_stats(0)
            first_norm(0)
            copy_normed(0)
            copy_keys(0)
            copy_queries(0, 0)
            run_stage_a(dve, stage_a)

            steps = Steps(dve, s_table)
            dve.wait_ge(s_count, 1)
            steps.then(nc.vector.tensor_tensor(count[:], work[:, 0, 0:EXPERTS], zeros[:, 0:EXPERTS], ALU.add))
            steps.then(nc.vector.scalar_tensor_tensor(pad_f[:], count[:], lane[:, 0:1], region_base[:], ALU.add, ALU.add))
            steps.then(nc.vector.tensor_copy(pad_rows[:], pad_f[:]))
            assert steps.n == PADS_MADE
            m = TOKENS // P
            dve.wait_ge(s_const, 9)
            steps.then(nc.vector.tensor_tensor(over, count[:].unsqueeze(2).broadcast_to([P, EXPERTS, m]), edges, ALU.is_gt))
            steps.then(nc.vector.reduce_sum(n_tiles[:], over, AX.X))
            steps.then(nc.vector.tensor_copy(tiles_to[:], n_tiles[0:1]))
            for e in range(1, EXPERTS):
                steps.then(nc.vector.tensor_tensor(tiles_to[:, e:e + 1], tiles_to[:, e - 1:e], n_tiles[0:1, e:e + 1], ALU.add))
            by_expert = [1, TABLE, EXPERTS]
            steps.then(nc.vector.tensor_tensor(past, tiles_to[:].unsqueeze(1).broadcast_to(by_expert),
                                               tile_no[:].unsqueeze(2).broadcast_to(by_expert), ALU.is_le))
            steps.then(nc.vector.reduce_sum(expert_f[:], past, AX.X))
            steps.then(nc.vector.tensor_tensor(past_tiles, past, n_tiles[0:1].unsqueeze(1).broadcast_to(by_expert), ALU.mult))
            steps.then(nc.vector.reduce_sum(skipped[:], past_tiles, AX.X))
            steps.then(nc.vector.tensor_tensor(row_f[:], tile_no[:], skipped[:], ALU.subtract))
            steps.then(nc.vector.tensor_scalar(skipped[:], expert_f[:], float(REGION), None, ALU.mult))
            steps.then(nc.vector.scalar_tensor_tensor(row_f[:], row_f[:], float(P), skipped[:], ALU.mult, ALU.add))
            steps.then(nc.vector.tensor_copy(row_table[:], row_f[:]))
            steps.then(nc.vector.tensor_scalar(expert_f[:], expert_f[:], float(EXPERTS - 1), None, ALU.min))
            steps.then(nc.vector.tensor_copy(expert_table[:], expert_f[:]))
            assert steps.n == TABLE_STEPS, steps.n
            steps.then(nc.vector.tensor_scalar(closer[:], n_tiles[:], float(P), -float(REGION), ALU.mult, ALU.add))
            for e in range(1, EXPERTS):
                steps.then(nc.vector.tensor_scalar(moved, slots_all[:], float(e * REGION), None, ALU.is_ge))
                steps.then(nc.vector.scalar_tensor_tensor(rows_f, moved, closer[:, e - 1:e], rows_f if e > 1 else slots_all[:], ALU.mult, ALU.add))
            steps.then(nc.vector.tensor_copy(y_rows[:], rows_f))
            assert steps.n == ROWS_MADE, steps.n

            def copy_tileT(t, u):
                dve.wait_ge(s_xt, t + 1)
                nc.vector.tensor_copy(xsT[:, u, :], swap[:, 0:DC * P]).then_inc(s_xtc, 1)

            def fuse(t, u):
                dve.wait_ge(s_silu, t + 1)
                dve.wait_ge(s_up, t + 1)
                nc.vector.tensor_tensor(fused[:, u, :], gated[:, u, :], score[:, 2 + u, :], ALU.mult).then_inc(s_fuse, 1)

            def copy_y(t, u):
                dve.wait_ge(s_down, t + 1)
                nc.vector.tensor_copy(ys[:, u, :], work[:, u, 0:D]).then_inc(s_y, 1)

            copy_tileT(0, 0)
            copy_tileT(1, 1)
            fuse(0, 0)

            def expert_tiles(tt, first):
                for v in range(2):
                    t, u = tt * 2 + v + 1, (1 + v) % 2
                    fuse(t, u)
                    if not first:
                        dve.wait_ge(s_ys[1 - u], tt * 16)
                    copy_tileT(t + 1, 1 - u)
                    copy_y(t - 1, 1 - u)

            expert_tiles(0, True)
            with dve.Fori(1, (TILES - 1) // 2) as tt:
                expert_tiles(tt, False)
            dve.wait_ge(s_ys[0], (TILES - 1) // 2 * 16)
            copy_y(TILES - 1, 0)

            def combine_groups(gg, first):
                for u in range(2):
                    g = gg * 2 + u
                    nc.vector.tensor_copy(mix[:, u, :], weights_all[:, bass.ds(g * 2 * GROUP, 2 * GROUP)]).then_inc(s_mix, 1)
                    dve.wait_ge(s_mix, g + 1)
                    dve.wait_ge(s_gather[u], gg * 128 + 128)
                    dve.wait_ge(s_r[u], gg * 16 + 16)
                    if not first:
                        dve.wait_ge(s_out[u], gg * 16)
                    for b in range(GROUP):
                        last = nc.vector.scalar_tensor_tensor(fin[:, u, b, :], y1[:, u, b, :], mix[:, u, b:b + 1],
                                                              res[:, u, b, :], ALU.mult, ALU.add)
                    last.then_inc(s_half, 1)
                    dve.wait_ge(s_half, g + 1)
                    for b in range(GROUP):
                        last = nc.vector.scalar_tensor_tensor(fin[:, u, b, :], y2[:, u, b, :], mix[:, u, GROUP + b:GROUP + b + 1],
                                                              fin[:, u, b, :], ALU.mult, ALU.add)
                    last.then_inc(s_comb[u], 1)

            combine_groups(0, True)
            with dve.Fori(1, GROUPS // 2) as gg:
                combine_groups(gg, False)


_INS = ['x', 'ctx_1024', 'L0_xattn_Wq', 'L0_xattn_bq', 'L0_xattn_Wk', 'L0_xattn_bk', 'L0_xattn_Wv', 'L0_xattn_bv',
        'L0_xattn_Wo', 'L0_xattn_bo', 'L0_ffn_kernel_router_DE', 'L0_ffn_kernel_gating_EDF',
        'L0_ffn_kernel_up_EDF', 'L0_ffn_kernel_down_EFD']


def kernel(**inputs):
    import numpy as _np
    import concourse.bacc as _bacc
    from concourse.bass_utils import run_bass_kernel_spmd as _run

    nc = _bacc.Bacc("TRN2", target_bir_lowering=False, num_devices=1)
    arrays, args = {}, []
    for name in _INS:
        a = _np.asarray(inputs[name])
        if name == 'ctx_1024':
            a = a.reshape(TOKENS, D).T
        a = _np.ascontiguousarray(a)
        arrays[f"in_{name}"] = a
        args.append(nc.dram_tensor(f"in_{name}", a.shape, mybir.dt.from_np(a.dtype), kind="ExternalInput").ap())
    out = nc.dram_tensor("out_0", (SEQS, TOK, D), mybir.dt.float32, kind="ExternalOutput").ap()
    moe_attention(nc, *args, out)
    r = _run(nc, [arrays], core_ids=[0])
    return r.results[0]["out_0"]
```

```python
from contextlib import ExitStack

import concourse.bass as bass
from concourse import mybir

P = 128
SEQS, TOK, D = 64, 128, 256
HEADS, DK = 16, 16
EXPERTS, F = 8, 512
GROUP = 4
GROUPS = SEQS // GROUP
DC = D // P
FC = F // P
QUADS = HEADS // 4
TOKENS = SEQS * TOK
REGION = TOKENS + P
USED_TILES = 2 * TOKENS // P + EXPERTS - 1
TILES = -(-(USED_TILES - 1) // 4) * 4 + 1
TABLE = TILES + 1
SPARE_TILES = TABLE - 2 * TOKENS // P
SPARE = EXPERTS * REGION
SORTED_ROWS = SPARE + SPARE_TILES * P
EPS = 1e-5
WEIGHTS, RANKS, TOKEN, ROW = D, D + 2, D + 4, D + 5
BLANKS = SPARE_TILES + 1


class Steps:

    def __init__(self, eng, sem, base=0, n=0):
        self.eng, self.sem, self.base, self.n = eng, sem, base, n

    def done(self, instruction):
        self.n += 1
        instruction.then_inc(self.sem, 1)

    def wait(self):
        self.eng.wait_ge(self.sem, self.base + self.n)

    def then(self, instruction):
        self.done(instruction)
        self.wait()


def moe_attention(nc, x, ctxT, wq, bq, wk, bk, wv, bv, wo, bo, router, gating, up, down, out):
    fp32, bf16 = mybir.dt.float32, mybir.dt.bfloat16
    u32, i32 = mybir.dt.uint32, mybir.dt.int32
    ACT, ALU, AX = mybir.ActivationFunctionType, mybir.AluOpType, mybir.AxisListType

    with ExitStack() as ctx:
        def sb(name, shape, dt=fp32):
            return ctx.enter_context(nc.sbuf_tensor(name, shape, dt))

        def sem(name):
            return ctx.enter_context(nc.semaphore(name))

        sorted_x = nc.dram_tensor("sorted_x", (SORTED_ROWS, ROW), fp32, kind="Internal").ap()

        wq_sb, wk_sb, wv_sb = (sb(n, [P, DC, D]) for n in ("wq_sb", "wk_sb", "wv_sb"))
        wo_sb = sb("wo_sb", [P, DC, D])
        wr_sb = sb("wr_sb", [P, DC, EXPERTS])
        bq_sb, bk_sb = sb("bq_sb", [P, DC]), sb("bk_sb", [P, DC])
        bv_sb, bo_sb = sb("bv_sb", [P, D]), sb("bo_sb", [P, D])
        gate_sb = sb("gate_sb", [P, EXPERTS * DC * F])
        up_sb = sb("up_sb", [P, EXPERTS * DC * F])
        down_sb = sb("down_sb", [P, EXPERTS * FC * D])
        ident = sb("ident", [P, P])
        before = sb("before", [P, P], bf16)
        ones = sb("ones", [P, P], bf16)
        head_rows = sb("head_rows", [P, 8])
        minus_half = sb("minus_half", [P, GROUP])
        region_base = sb("region_base", [P, EXPERTS])
        first_rank = sb("first_rank", [P, EXPERTS])
        blank = sb("blank", [P, ROW])

        x_sb = sb("x_sb", [P, GROUP, D])
        x_bo = sb("x_bo", [P, 2, GROUP, D])
        ctxT_sb = sb("ctxT_sb", [P, DC, GROUP * TOK])
        stats = sb("stats", [P, GROUP, 6])
        mean_var = sb("mean_var", [P, GROUP, 2])
        var_eps, var_eps2, rstd, rstd2 = (sb(n, [P, GROUP]) for n in ("var_eps", "var_eps2", "rstd", "rstd2"))
        xn = sb("xn", [P, GROUP, D])
        xnT = sb("xnT", [P, DC, GROUP * TOK])
        qT = sb("qT", [P, 2, DC, GROUP * TOK])
        kT = sb("kT", [P, DC, GROUP * TOK])
        k_blocks = sb("k_blocks", [P, 2, QUADS, 4 * TOK])
        v_aug = sb("v_aug", [P, GROUP, HEADS, 32])
        row_max = sb("row_max", [P, 2, 8])
        probs = sb("probs", [P, 2, 8, TOK])
        probsT = sb("probsT", [P, 2, 4 * TOK])
        attT = sb("attT", [P, QUADS * TOK])
        inv_sum = sb("inv_sum", [P, HEADS])
        attn = sb("attn", [P, D])
        attnT = sb("attnT", [P, D])
        x1 = sb("x1", [P, GROUP, D])
        xn2 = sb("xn2", [P, GROUP, ROW])
        xn2T = xnT
        GE = [P, GROUP, EXPERTS]
        logits, prob, tied, rest, pick1, pick2, place, picked = (
            sb(n, GE) for n in ("logits", "prob", "tied", "rest", "pick1", "pick2", "place", "picked"))
        best, total, top1, top2, gap, share = (
            sb(n, [P, GROUP]) for n in ("best", "total", "top1", "top2", "gap", "share"))
        chosen = sb("chosen", GE, bf16)
        chosen_f = sb("chosen_f", GE)
        seen = sb("seen", [P, GROUP + 1, EXPERTS])
        seen_bf = sb("seen_bf", [P, GROUP + 1, EXPERTS], bf16)
        slot_f = sb("slot_f", [P, 2 * GROUP])
        slots_now = sb("slots_now", [P, 2 * GROUP], u32)

        lane = sb("lane", [P, 1])
        count = sb("count", [P, EXPERTS])
        pad_f = sb("pad_f", [P, EXPERTS])
        pad_rows = sb("pad_rows", [P, EXPERTS], u32)
        tile_no = sb("tile_no", [P, TABLE])
        n_tiles = sb("n_tiles", [P, EXPERTS])
        tiles_to = sb("tiles_to", [P, EXPERTS])
        table_room = k_blocks[:].rearrange("p u q t -> p (u q t)")
        past, past_tiles = (
            table_room[:, i * TABLE * EXPERTS:(i + 1) * TABLE * EXPERTS].rearrange("p (a b) -> p a b", b=EXPERTS)
            for i in range(2))
        over, edges = (
            table_room[:, 3072 + i * TOKENS // 16:3072 + (i + 1) * TOKENS // 16].rearrange("p (e m) -> p e m", e=EXPERTS)
            for i in range(2))
        expert_f, skipped, row_f = (sb(n, [P, TABLE]) for n in ("expert_f", "skipped", "row_f"))
        tile_rank = sb("tile_rank", [P, TABLE])
        row_table = sb("row_table", [1, TABLE], i32)
        expert_table = sb("expert_table", [1, TABLE], i32)

        xs = x_bo[:].rearrange("p u s d -> p u (s d)")[:, :, 0:ROW]
        xsT = xnT[:, :, 0:DC * P]
        gated, fused = qT[:, 0], kT
        fusedT = probs[:].rearrange("p u h t -> p u (h t)")[:, :, 0:F]
        ys = xn[:, 0:2, :]
        pair = sb("pair", [P, 2])
        weight = sb("weight", [P, 4, 1])
        token = sb("token", [P, 4, 1], u32)

        score = ctx.enter_context(nc.psum_tensor("score", [P, 4, 512], fp32))
        swap = ctx.enter_context(nc.psum_tensor("swap", [P, 512], fp32))
        att = ctx.enter_context(nc.psum_tensor("att", [P, 512], fp32))
        work = ctx.enter_context(nc.psum_tensor("work", [P, 2, 512], fp32))

        s_wkvq, s_bias, s_wo, s_experts = (sem(n) for n in ("wkvq_loaded", "bias_loaded", "wo_loaded", "experts_loaded"))
        s_x, s_ctx, s_xbo = sem("x_loaded"), sem("ctx_loaded"), sem("x_bo_ready")
        s_kb = sem("keys_placed")
        s_res, s_scat, s_pad = (sem(n) for n in ("resid_stored", "rows_written", "pads_written"))
        s_zero, s_masks, s_const = (sem(n) for n in ("zeroed", "masks_ready", "consts_ready"))
        s_ln, s_rstd, s_norm = (sem(n) for n in ("ln1_steps", "rstd_ready", "x_normed"))
        s_front, s_front_v, s_front_a = (sem(n) for n in ("front_product", "front_copied_by_vector", "front_copied_by_scalar"))
        s_score, s_max, s_shift, s_exp = (sem(n) for n in ("scores_ready", "row_max_ready", "scores_shifted", "probs_ready"))
        s_swap, s_probsT, s_att, s_attT = (sem(n) for n in ("probs_swapped", "probsT_ready", "att_product", "attT_ready"))
        s_back, s_inv, s_attn = (sem(n) for n in ("att_swapped_back", "inverse_sums_ready", "attn_normalised"))
        s_fwd, s_attnT = sem("attn_swapped"), sem("attnT_ready")
        s_proj, s_x1 = sem("projected"), sem("x1_ready")
        s_rstd2, s_norm2 = sem("rstd2_ready"), sem("x1_normed")
        s_n2T, s_n2Tv, s_n2Ta = (sem(n) for n in ("x1_swapped", "x1T_copied_by_vector", "x1T_copied_by_scalar"))
        s_logit, s_route, s_lexp, s_gexp = (sem(n) for n in ("logits_ready", "route_steps", "router_exp_ready", "gap_exp_ready"))
        s_place = sem("places_ready")
        s_count, s_table = sem("counts_ready"), sem("table_steps")
        s_xs = [sem("tile_loaded_0"), sem("tile_loaded_1")]
        s_pair, s_meta, s_acc = sem("row_weights_masked"), sem("row_weights_ready"), sem("tile_added")
        s_xt, s_xtc, s_gate, s_up, s_silu, s_fuse = (sem(n) for n in (
            "tile_swapped", "tileT_ready", "gate_product", "up_product", "silu_ready", "fused_ready"))
        s_ft, s_ftc, s_down, s_y = (sem(n) for n in ("fused_swapped", "fusedT_ready", "down_product", "y_ready"))

        LN_STEPS = 3
        ROUTE_STEPS = 38
        SHIFTED = 5
        GAP = 20
        CHOSEN = 27
        PLACES_READ = 29
        TABLE_STEPS = 24
        PADS_MADE = 3

        block = ctx.enter_context(nc.Block())

        def wait(eng, semaphore, value):
            if not isinstance(value, int) or value > 0:
                eng.wait_ge(semaphore, value)

        def run_stage_a(eng, group):
            def at(g):
                group(g, g < GROUPS, 1 <= g <= GROUPS, g >= 2, g + 1 < GROUPS, g + 2 < GROUPS)

            at(0)
            at(1)
            with eng.Fori(1, GROUPS // 2 - 1) as pair:
                for u in range(2):
                    group(pair * 2 + u, True, True, True, True, True)
            for g in range(GROUPS - 2, GROUPS + 2):
                at(g)

        @block.sync
        def _(sp):
            def load_x(g):
                sp.dma_start(x_sb[:], x[bass.ds(g * GROUP, GROUP)].rearrange("s t d -> t s d")).then_inc(s_x, 16)

            def load_ctx(g):
                sp.dma_start(ctxT_sb[:], ctxT[:, bass.ds(g * GROUP * TOK, GROUP * TOK)].rearrange(
                    "(c p) t -> p c t", p=P)).then_inc(s_ctx, 16)

            load_x(0)
            load_ctx(0)
            for w_sb, w in ((wk_sb, wk), (wv_sb, wv), (wq_sb, wq)):
                sp.dma_start(w_sb[:], w.rearrange("(c p) n -> p c n", p=P)).then_inc(s_wkvq, 16)
            for b_sb, b in ((bk_sb, bk), (bq_sb, bq)):
                sp.dma_start(b_sb[:], b.rearrange("(c p) -> p c", p=P), allow_slow_non_contiguous=True).then_inc(s_bias, 16)
            for b_sb, b in ((bv_sb, bv), (bo_sb, bo)):
                sp.dma_start(b_sb[:], b.partition_broadcast(P)).then_inc(s_bias, 16)
            sp.dma_start(wo_sb[:], wo.rearrange("(c p) n -> p c n", p=P)).then_inc(s_wo, 16)
            sp.dma_start(wr_sb[:], router.rearrange("(c p) e -> p c e", p=P)).then_inc(s_wo, 16)
            for e in range(EXPERTS):
                for w_sb, w, c in ((gate_sb, gating, DC), (up_sb, up, DC), (down_sb, down, FC)):
                    n = w_sb.shape[1] // EXPERTS
                    sp.dma_start(w_sb[:, e * n:(e + 1) * n].rearrange("p (c f) -> p c f", c=c),
                                 w[e].rearrange("(c p) f -> p c f", p=P)).then_inc(s_experts, 16)
            sp.wait_ge(s_norm, 1)
            sp.wait_ge(s_xbo, 1)
            load_x(1)

            def stage_a(g, core, prev, prev2, nxt, far):
                if nxt:
                    wait(sp, s_front, g * 8 + 8)
                    load_ctx(g + 1)
                if prev:
                    wait(sp, s_x1, g * GROUP)
                    sp.dma_start(out[bass.ds((g - 1) * GROUP * TOK, GROUP * TOK)].rearrange("(s t) d -> t s d", t=TOK),
                                 x1[:]).then_inc(s_res, 16)
                if far:
                    wait(sp, s_xbo, g + 2)
                    load_x(g + 2)

            run_stage_a(sp, stage_a)

            sp.wait_ge(s_table, TABLE_STEPS)
            sp.wait_ge(s_scat, BLANKS * 16 + GROUPS * 2 * GROUP * 16)
            sp.wait_ge(s_pad, EXPERTS * 16)

            def row_of(t):
                return sp.value_load(row_table[0:1, bass.ds(t, 1)], min_val=0, max_val=SORTED_ROWS - P)

            def load_tile(t, u):
                sp.dma_start(xs[:, u, :], sorted_x[bass.ds(row_of(t), P), :]).then_inc(s_xs[u], 16)

            load_tile(0, 0)
            load_tile(1, 1)
            with sp.Fori(0, (TILES - 1) // 2) as tt:
                for u in range(2):
                    t = tt * 2 + u
                    sp.wait_ge(s_xt, t + 1)
                    sp.wait_ge(s_meta, t + 1)
                    load_tile(t + 2, u)

        @block.gpsimd
        def _(pool):
            nc.gpsimd.memset(head_rows[:], 1.0).then_inc(s_zero, 1)
            nc.gpsimd.memset(ident[:], 0.0).then_inc(s_zero, 1)
            nc.gpsimd.memset(before[:], 1.0).then_inc(s_zero, 1)
            nc.gpsimd.memset(v_aug[:], 0.0).then_inc(s_zero, 1)
            pool.wait_ge(s_zero, 4)
            nc.gpsimd.affine_select(out=ident[:], in_=ident[:], compare_op=ALU.not_equal, fill=1.0, base=0,
                                    pattern=[[-1, P]], channel_multiplier=1).then_inc(s_masks, 1)
            nc.gpsimd.affine_select(out=before[:], in_=before[:], compare_op=ALU.is_gt, fill=0.0, base=0,
                                    pattern=[[1, P]], channel_multiplier=-1).then_inc(s_masks, 1)
            nc.gpsimd.memset(v_aug[:, :, :, DK:DK + 1], 1.0).then_inc(s_masks, 1)
            nc.gpsimd.affine_select(out=head_rows[:], in_=head_rows[:], compare_op=ALU.is_ge, fill=0.0, base=0,
                                    pattern=[[-DK, 8]], channel_multiplier=1).then_inc(s_masks, 1)
            pool.wait_ge(s_masks, 4)
            nc.gpsimd.affine_select(out=head_rows[:], in_=head_rows[:], compare_op=ALU.is_gt, fill=0.0, base=DK,
                                    pattern=[[DK, 8]], channel_multiplier=-1).then_inc(s_masks, 1)
            nc.gpsimd.memset(minus_half[:], -0.5).then_inc(s_const, 1)
            nc.gpsimd.memset(ones[:], 1.0).then_inc(s_const, 1)
            nc.gpsimd.memset(blank[:, 0:TOKEN], 0.0).then_inc(s_const, 1)
            nc.gpsimd.memset(seen[:], 0.0).then_inc(s_const, 1)
            small = dict(allow_small_or_imprecise_dtypes=True)
            nc.gpsimd.iota(region_base[:], pattern=[[REGION, EXPERTS]], base=0, channel_multiplier=0, **small).then_inc(s_const, 1)
            nc.gpsimd.iota(first_rank[:], pattern=[[-1, EXPERTS]], base=EXPERTS, channel_multiplier=0, **small).then_inc(s_const, 1)
            nc.gpsimd.iota(lane[:], pattern=[[0, 1]], base=0, channel_multiplier=1, **small).then_inc(s_const, 1)
            nc.gpsimd.iota(tile_no[:], pattern=[[1, TABLE]], base=0, channel_multiplier=0, **small).then_inc(s_const, 1)
            nc.gpsimd.iota(blank[:, TOKEN:ROW], pattern=[[0, 1]], base=TOKENS, channel_multiplier=1, **small).then_inc(s_const, 1)
            nc.gpsimd.iota(xn2[:, :, TOKEN], pattern=[[TOK, GROUP]], base=-GROUP * TOK, channel_multiplier=1, **small).then_inc(s_const, 1)
            pool.wait_ge(s_const, 10)
            for i in range(SPARE_TILES):
                pool.dma_start(sorted_x[SPARE + i * P:SPARE + (i + 1) * P, :], blank[:]).then_inc(s_scat, 16)
            pool.dma_start(out[TOKENS:TOKENS + P, :], blank[:, 0:D]).then_inc(s_scat, 16)

            def place_keys(g, b):
                wait(pool, s_score, g * 16 + 4 * b - 4)
                for c in range(DC):
                    nc.gpsimd.tensor_tensor(
                        k_blocks[:, b % 2, 2 * c:2 * c + 2, :].rearrange("p q (h t) -> p (q h) t", t=TOK),
                        kT[:, c, b * TOK:(b + 1) * TOK].unsqueeze(1).broadcast_to([P, 8, TOK]),
                        head_rows[:].unsqueeze(2).broadcast_to([P, 8, TOK]), ALU.mult).then_inc(s_kb, 1)

            def root(g):
                wait(pool, s_ln, g * LN_STEPS + LN_STEPS)
                nc.gpsimd.tensor_tensor(rstd[:], var_eps[:], minus_half[:], ALU.pow).then_inc(s_rstd, 1)

            def keep_x(g, u, first):
                wait(pool, s_norm, g + 1)
                if not first:
                    wait(pool, s_x1, (g - 1) * GROUP)
                nc.gpsimd.tensor_tensor(x_bo[:, u], x_sb[:], bo_sb[:].unsqueeze(1).broadcast_to([P, GROUP, D]),
                                        ALU.add).then_inc(s_xbo, 1)

            def first_keys(g):
                wait(pool, s_front_v, g * 5 + 2)
                wait(pool, s_front_a, g * 3 + 2)
                place_keys(g, 0)
                place_keys(g, 1)

            rounds = iter([0, 1, 0, 1, 0, 1, 0, 1])

            def stage_a(g, core, prev, prev2, nxt, far):
                u = next(rounds)
                if core:
                    place_keys(g, 2)
                if nxt:
                    root(g + 1)
                if core:
                    place_keys(g, 3)
                if prev2:
                    wait(pool, s_route, (g - 2) * ROUTE_STEPS + ROUTE_STEPS)
                    pool.nop(nofuse=True)
                    for i in range(2 * GROUP):
                        pool.indirect_dma_start(
                            out=sorted_x[:, :], out_offset=bass.IndirectOffsetOnAxis(ap=slots_now[:, i:i + 1], axis=0),
                            in_=xn2[:, i % GROUP, :], in_offset=None).then_inc(s_scat, 16)
                if prev:
                    wait(pool, s_route, (g - 1) * ROUTE_STEPS + LN_STEPS)
                    nc.gpsimd.tensor_tensor(rstd2[:], var_eps2[:], minus_half[:], ALU.pow).then_inc(s_rstd2, 1)
                if nxt:
                    keep_x(g + 1, 1 - u, False)
                    first_keys(g + 1)

            pool.wait_ge(s_bias, 64)
            root(0)
            keep_x(0, 0, True)
            first_keys(0)
            run_stage_a(pool, stage_a)
            small = dict(allow_small_or_imprecise_dtypes=True)
            nc.gpsimd.iota(edges, pattern=[[0, EXPERTS], [P, TOKENS // P]], base=0, channel_multiplier=0, **small).then_inc(s_const, 1)
            pool.wait_ge(s_table, PADS_MADE)
            for e in range(EXPERTS):
                pool.indirect_dma_start(
                    out=sorted_x[:, :], out_offset=bass.IndirectOffsetOnAxis(ap=pad_rows[:, e:e + 1], axis=0),
                    in_=blank[:], in_offset=None).then_inc(s_pad, 16)

            pool.wait_ge(s_res, GROUPS * 16)
            pool.wait_ge(s_scat, BLANKS * 16)

            def add_tile(t, u, v):
                pool.wait_ge(s_y, t + 1)
                pool.nop(nofuse=True)
                pool.indirect_dma_start(
                    out=out[:, :], out_offset=bass.IndirectOffsetOnAxis(ap=token[:, v, :], axis=0),
                    in_=ys[:, u, :], in_offset=None, compute_op=ALU.add).then_inc(s_acc, 16)

            add_tile(0, 0, 0)
            with pool.Fori(0, (TILES - 1) // 4) as tt:
                for v in range(4):
                    t = tt * 4 + v + 1
                    pool.wait_ge(s_acc, t * 16)
                    add_tile(t, (v + 1) % 2, (v + 1) % 4)
            pool.wait_ge(s_acc, TILES * 16)

        @block.tensor
        def _(pe):
            def product(dst, pairs):
                for i, (lhsT, rhs) in enumerate(pairs):
                    last = nc.tensor.matmul(dst, lhsT, rhs, start=(i == 0), stop=(i == len(pairs) - 1))
                return last

            banks = {"qT": iter([0, 1, 0, 1, 0, 1, 0, 1])}

            def norm_swapped(g, c):
                wait(pe, s_norm, g + 1)
                if c == 1:
                    wait(pe, s_front_v, g * 5 + 1)
                for b in range(GROUP):
                    last = nc.tensor.transpose(work[:, 0, b * P:(b + 1) * P], xn[:, b, c * P:(c + 1) * P], ident[:])
                last.then_inc(s_front, 1)

            def keys(g, m):
                wait(pe, s_ctx, g * 16 + 16)
                product(work[:, m, :], [(wk_sb[:, c, m * P:(m + 1) * P], ctxT_sb[:, c, :]) for c in range(DC)]).then_inc(s_front, 1)

            def queries(g, m):
                wait(pe, s_front_v, g * 5 + 2 + m)
                wait(pe, s_front_a, g * 3 + 1)
                product(work[:, 0, :], [(wq_sb[:, c, m * P:(m + 1) * P], xnT[:, c, :]) for c in range(DC)]).then_inc(s_front, 1)

            def values(g, m):
                for s in range(2):
                    t = (2 * m + s) * TOK
                    last = product(work[:, m, s * D:(s + 1) * D], [(ctxT_sb[:, c, t:t + TOK], wv_sb[:, c, :]) for c in range(DC)])
                last.then_inc(s_front, 1)

            def scores(g, u, k):
                b, c = k // 2, k % 2
                if k == 0:
                    wait(pe, s_front_v, g * 5 + 3)
                    wait(pe, s_front_a, g * 3 + 3)
                wait(pe, s_shift, g * 8 + k - 1)
                wait(pe, s_kb, g * 8 + k + 1)
                for q in (2 * c, 2 * c + 1):
                    nc.tensor.matmul(score[:, q, :], qT[:, u, c, b * TOK:(b + 1) * TOK], k_blocks[:, b % 2, q, :],
                                     start=True, stop=True).then_inc(s_score, 1)

            def swap_probs(g, n):
                c = n // 2 % 2
                wait(pe, s_exp, g * 8 + n // 2 + 1)
                wait(pe, s_probsT, g * 16 + n)
                for j in range(4):
                    last = nc.tensor.transpose(swap[:, j * TOK:(j + 1) * TOK], probs[:, c, 4 * (n % 2) + j, :], ident[:])
                last.then_inc(s_swap, 1)

            def attend(g, n):
                b, q = n // 4, n % 4
                wait(pe, s_probsT, g * 16 + n + 1)
                if n == 0:
                    wait(pe, s_front_v, g * 5 + 5)
                if q == 0:
                    wait(pe, s_attT, g * 4 + b)
                for j in range(4):
                    last = nc.tensor.matmul(att[32 * j:32 * j + 32, q * TOK:(q + 1) * TOK], v_aug[:, b, 4 * q + j, :],
                                            probsT[:, n % 2, j * TOK:(j + 1) * TOK], start=True, stop=True)
                last.then_inc(s_att, 1)

            def swap_back(i):
                wait(pe, s_attT, i + 1)
                wait(pe, s_attn, i)
                for q in range(QUADS):
                    last = nc.tensor.transpose(work[:, 0, q * TOK:(q + 1) * TOK], attT[:, q * TOK:(q + 1) * TOK], ident[:])
                last.then_inc(s_back, 1)

            def swap_forth(i):
                wait(pe, s_attn, i + 1)
                wait(pe, s_x1, i)
                for c in range(DC):
                    last = nc.tensor.transpose(work[:, 1, c * P:(c + 1) * P], attn[:, c * P:(c + 1) * P], ident[:])
                last.then_inc(s_fwd, 1)

            def project(i):
                wait(pe, s_attnT, i + 1)
                product(work[:, 1, 0:D], [(attnT[:, c * P:(c + 1) * P], wo_sb[:, c, :]) for c in range(DC)]).then_inc(s_proj, 1)

            def x1_swapped(g, c):
                if c == 0:
                    wait(pe, s_norm2, g + 1)
                else:
                    wait(pe, s_n2Tv, g + 1)
                for b in range(GROUP):
                    last = nc.tensor.transpose(work[:, 0, b * P:(b + 1) * P], xn2[:, b, c * P:(c + 1) * P], ident[:])
                last.then_inc(s_n2T, 1)

            def route_logits(g):
                wait(pe, s_n2Ta, g + 1)
                for b in range(GROUP):
                    last = product(work[:, 0, b * EXPERTS:(b + 1) * EXPERTS],
                                   [(xn2T[:, c, b * TOK:(b + 1) * TOK], wr_sb[:, c, :]) for c in range(DC)])
                last.then_inc(s_logit, 1)

            def places(g):
                wait(pe, s_route, g * ROUTE_STEPS + CHOSEN)
                for b in range(GROUP):
                    last = product(work[:, 1, b * EXPERTS:(b + 1) * EXPERTS],
                                   [(before[:], chosen[:, b, :]), (ones[:], seen_bf[:, b, :])])
                last.then_inc(s_place, 1)

            def stage_a(g, core, prev, prev2, nxt, far):
                u = next(banks["qT"])
                old = (g - 1) * GROUP
                for k in range(8):
                    if core and k < 6:
                        scores(g, u, k + 2)
                    elif nxt:
                        scores(g + 1, 1 - u, k - 6)
                    if k == 0 and core:
                        wait(pe, s_attn, g * GROUP - 1)
                        values(g, 0)
                        wait(pe, s_x1, g * GROUP - 2)
                        values(g, 1)
                    if k == 3 and nxt:
                        norm_swapped(g + 1, 1)
                    if k == 3 and prev2:
                        if prev:
                            wait(pe, s_attnT, g * GROUP)
                        places(g - 2)
                    if k == 4 and nxt:
                        wait(pe, s_attn, g * GROUP + 1)
                        keys(g + 1, 0)
                        wait(pe, s_x1, g * GROUP)
                        keys(g + 1, 1)
                    if k == 5 and nxt:
                        queries(g + 1, 1)
                    if k == 6 and prev:
                        wait(pe, s_attn, g * GROUP + 2 if core else g * GROUP)
                        x1_swapped(g - 1, 0)
                    if k == 7 and prev:
                        x1_swapped(g - 1, 1)
                    if core:
                        swap_probs(g, 2 * k)
                        swap_probs(g, 2 * k + 1)
                        attend(g, 2 * k)
                        attend(g, 2 * k + 1)
                    if k == 0:
                        if prev:
                            swap_forth(old + 2)
                        if prev2:
                            wait(pe, s_attn, g * GROUP - 1 if prev else SEQS)
                            route_logits(g - 2)
                    if k == 1 and prev:
                        project(old + 2)
                        if prev2:
                            wait(pe, s_route, (g - 2) * ROUTE_STEPS + SHIFTED)
                        swap_back(old + 3)
                    if k == 2:
                        if prev:
                            swap_forth(old + 3)
                        if nxt:
                            wait(pe, s_attn, g * GROUP)
                            norm_swapped(g + 1, 0)
                    if k == 3:
                        if prev:
                            if prev2:
                                wait(pe, s_route, (g - 2) * ROUTE_STEPS + PLACES_READ)
                            project(old + 3)
                        if core:
                            if nxt:
                                wait(pe, s_front_a, g * 3 + 4)
                            swap_back(g * GROUP)
                    if k == 4:
                        if core:
                            if nxt:
                                wait(pe, s_front_a, g * 3 + 5)
                            swap_forth(g * GROUP)
                        if nxt:
                            queries(g + 1, 0)
                    if k == 5 and core:
                        project(g * GROUP)
                        if nxt:
                            wait(pe, s_front_a, g * 3 + 6)
                        swap_back(g * GROUP + 1)
                    if k == 6 and core:
                        swap_forth(g * GROUP + 1)
                    if k == 7 and core:
                        project(g * GROUP + 1)
                        if prev:
                            wait(pe, s_n2Ta, g)
                        swap_back(g * GROUP + 2)

            pe.wait_ge(s_wkvq, 48)
            pe.wait_ge(s_masks, 5)
            pe.wait_ge(s_const, 8)
            pe.wait_ge(s_wo, 32)
            norm_swapped(0, 0)
            norm_swapped(0, 1)
            pe.wait_ge(s_front_a, 1)
            keys(0, 0)
            keys(0, 1)
            queries(0, 0)
            queries(0, 1)
            scores(0, 0, 0)
            scores(0, 0, 1)
            run_stage_a(pe, stage_a)
            pe.wait_ge(s_route, GROUPS * ROUTE_STEPS)
            nc.tensor.matmul(work[:, 0, 0:EXPERTS], ones[:], seen_bf[:, GROUP, :], start=True, stop=True).then_inc(s_count, 1)

            def swap_tile(t, u, loads):
                pe.wait_ge(s_xs[u], loads * 16)
                pe.wait_ge(s_xtc, t)
                for c in range(DC):
                    last = nc.tensor.transpose(swap[:, c * P:(c + 1) * P], xs[:, u, c * P:(c + 1) * P], ident[:])
                last.then_inc(s_xt, 1)

            def expert_of(t):
                return pe.value_load(expert_table[0:1, bass.ds(t, 1)], min_val=0, max_val=EXPERTS - 1)

            def gate(t, u, e):
                pe.wait_ge(s_xtc, t + 1)
                product(score[:, u, :], [(xsT[:, u, c * P:(c + 1) * P], gate_sb[:, bass.ds(e * (DC * F) + c * F, F)])
                                         for c in range(DC)]).then_inc(s_gate, 1)

            def up_(t, u, e):
                product(score[:, 2 + u, :], [(xsT[:, u, c * P:(c + 1) * P], up_sb[:, bass.ds(e * (DC * F) + c * F, F)])
                                             for c in range(DC)]).then_inc(s_up, 1)

            def swap_fused(t, u):
                pe.wait_ge(s_fuse, t + 1)
                for c in range(FC):
                    last = nc.tensor.transpose(att[:, c * P:(c + 1) * P], fused[:, u, c * P:(c + 1) * P], ident[:])
                last.then_inc(s_ft, 1)

            def down_(t, u, e):
                pe.wait_ge(s_ftc, t + 1)
                product(work[:, u, 0:D], [(fusedT[:, u, c * P:(c + 1) * P], down_sb[:, bass.ds(e * (FC * D) + c * D, D)])
                                          for c in range(FC)]).then_inc(s_down, 1)

            pe.wait_ge(s_experts, EXPERTS * 3 * 16)
            pe.wait_ge(s_table, TABLE_STEPS)
            swap_tile(0, 0, 1)
            e = expert_of(0)
            gate(0, 0, e)
            up_(0, 0, e)
            swap_tile(1, 1, 1)

            with pe.Fori(0, (TILES - 1) // 4) as tt:
                for v in range(4):
                    t = tt * 4 + v + 1
                    u = (1 + v) % 2
                    e, e_last = expert_of(t), expert_of(t - 1)
                    pe.wait_ge(s_silu, t)
                    gate(t, u, e)
                    swap_fused(t - 1, 1 - u)
                    up_(t, u, e)
                    swap_tile(t + 1, 1 - u, tt * 2 + v // 2 + 2)
                    down_(t - 1, 1 - u, e_last)
            e = expert_of(TILES - 1)
            swap_fused(TILES - 1, 0)
            down_(TILES - 1, 0, e)

        @block.scalar
        def _(act):
            def copy_front(g, i):
                wait(act, s_front, g * 8 + (2, 4, 6)[i])
                if i == 0:
                    nc.scalar.activation(xnT[:, 1, :], work[:, 0, :], ACT.Copy).then_inc(s_front_a, 1)
                elif i == 1:
                    wait(act, s_kb, g * 8)
                    nc.scalar.activation(kT[:, 1, :], work[:, 1, :], ACT.Identity, bias=bk_sb[:, 1:2]).then_inc(s_front_a, 1)

            def copy_queries(g, u):
                wait(act, s_front, g * 8 + 6)
                nc.scalar.activation(qT[:, u, 1, :], work[:, 0, :], ACT.Identity, bias=bq_sb[:, 1:2]).then_inc(s_front_a, 1)

            def softmax_exp(g, k):
                wait(act, s_shift, g * 8 + k + 1)
                nc.scalar.activation(probs[:, k % 2], probs[:, k % 2], ACT.Exp, scale=DK ** -0.5).then_inc(s_exp, 1)

            def copy_probsT(g, n):
                wait(act, s_swap, g * 16 + n + 1)
                wait(act, s_att, g * 16 + n - 1)
                nc.scalar.activation(probsT[:, n % 2], swap[:], ACT.Copy).then_inc(s_probsT, 1)

            def copy_attT(i):
                wait(act, s_att, i * QUADS + QUADS)
                wait(act, s_back, i)
                nc.scalar.activation(attT[:], att[:], ACT.Copy).then_inc(s_attT, 1)

            def copy_attnT(i):
                wait(act, s_fwd, i + 1)
                nc.scalar.activation(attnT[:], work[:, 1, 0:D], ACT.Copy).then_inc(s_attnT, 1)

            rounds = iter([0, 1, 0, 1, 0, 1, 0, 1])

            def stage_a(g, core, prev, prev2, nxt, far):
                u = next(rounds)
                old = (g - 1) * GROUP
                for k in range(8):
                    if core:
                        softmax_exp(g, k)
                    if k in (1, 3) and prev:
                        copy_attnT(old + 2 + k // 2)
                    if k in (5, 7) and core:
                        copy_attnT(g * GROUP + (k - 5) // 2)
                    if k == 3 and nxt:
                        copy_front(g + 1, 0)
                    if k == 4 and nxt:
                        copy_front(g + 1, 1)
                    if k == 5 and nxt:
                        copy_queries(g + 1, 1 - u)
                    if k == 7 and prev:
                        wait(act, s_n2T, (g - 1) * 2 + 2)
                        nc.scalar.activation(xn2T[:, 1, :], work[:, 0, :], ACT.Copy).then_inc(s_n2Ta, 1)
                    if core:
                        copy_probsT(g, 2 * k)
                        copy_probsT(g, 2 * k + 1)
                    if k % 2 == 1 and core:
                        copy_attT(g * GROUP + k // 2)
                    if k == 1 and prev2:
                        wait(act, s_route, (g - 2) * ROUTE_STEPS + SHIFTED)
                        nc.scalar.activation(prob[:], logits[:], ACT.Exp).then_inc(s_lexp, 1)
                    if k == 2 and prev2:
                        wait(act, s_route, (g - 2) * ROUTE_STEPS + GAP)
                        nc.scalar.activation(gap[:], gap[:], ACT.Exp).then_inc(s_gexp, 1)

            act.wait_ge(s_bias, 64)
            copy_front(0, 0)
            copy_front(0, 1)
            copy_queries(0, 0)
            run_stage_a(act, stage_a)

            def silu(t, u):
                act.wait_ge(s_gate, t + 1)
                nc.scalar.activation(gated[:, u, :], score[:, u, :], ACT.Silu).then_inc(s_silu, 1)

            def copy_fusedT(t, u):
                act.wait_ge(s_ft, t + 1)
                nc.scalar.activation(fusedT[:, u, :], att[:], ACT.Copy).then_inc(s_ftc, 1)

            silu(0, 0)
            with act.Fori(0, (TILES - 1) // 4) as tt:
                for v in range(4):
                    t, u = tt * 4 + v + 1, (1 + v) % 2
                    silu(t, u)
                    copy_fusedT(t - 1, 1 - u)
            copy_fusedT(TILES - 1, 0)

        @block.vector
        def _(dve):
            def norm_stats(steps, src, eps_out):
                for b in range(GROUP):
                    last = nc.vector.bn_stats(stats[:, b, :], src[:, b, :])
                steps.then(last)
                dve.nop(nofuse=True)
                for b in range(GROUP):
                    last = nc.vector.bn_aggr(mean_var[:, b, :], stats[:, b, :])
                steps.then(last)
                steps.then(nc.vector.tensor_scalar(eps_out[:], mean_var[:, :, 1], EPS, None, ALU.add))

            def normalise(dst, src, scale, signal):
                for b in range(GROUP):
                    last = nc.vector.tensor_scalar(dst[:, b, 0:D], src[:, b, :], mean_var[:, b, 0:1], scale[:, b:b + 1],
                                                   ALU.subtract, ALU.mult)
                last.then_inc(signal, 1)

            def over_experts(col):
                return col.unsqueeze(2).broadcast_to([P, GROUP, EXPERTS])

            def over_group(row):
                return row[:].unsqueeze(1).broadcast_to([P, GROUP, EXPERTS])

            def first_best(steps, values, top, pick, rank):
                steps.then(nc.vector.reduce_max(top[:], values[:], AX.X))
                steps.then(nc.vector.tensor_tensor(tied[:], values[:], over_experts(top[:]), ALU.is_equal))
                steps.then(nc.vector.tensor_tensor(tied[:], tied[:], over_group(first_rank), ALU.mult))
                steps.then(nc.vector.reduce_max(rank, tied[:], AX.X))
                steps.then(nc.vector.tensor_tensor(pick[:], tied[:], over_experts(rank), ALU.is_equal))

            def first_norm_stats(g):
                wait(dve, s_x, g * 16 + 16)
                norm_stats(Steps(dve, s_ln, g * LN_STEPS), x_sb, var_eps)

            def first_norm(g):
                wait(dve, s_rstd, g + 1)
                normalise(xn, x_sb, rstd, s_norm)

            def copy_normed(g):
                wait(dve, s_front, g * 8 + 1)
                nc.vector.tensor_copy(xnT[:, 0, :], work[:, 0, :]).then_inc(s_front_v, 1)

            def copy_keys(g):
                wait(dve, s_front, g * 8 + 3)
                wait(dve, s_kb, g * 8)
                nc.vector.tensor_scalar(kT[:, 0, :], work[:, 0, :], bk_sb[:, 0:1], None, ALU.add).then_inc(s_front_v, 1)

            def copy_queries(g, u):
                wait(dve, s_front, g * 8 + 5)
                nc.vector.tensor_scalar(qT[:, u, 0, :], work[:, 0, :], bq_sb[:, 0:1], None, ALU.add).then_inc(s_front_v, 1)

            def copy_values(g):
                for m in range(2):
                    wait(dve, s_front, g * 8 + 7 + m)
                    for s in range(2):
                        last = nc.vector.tensor_tensor(
                            v_aug[:, 2 * m + s, :, 0:DK], work[:, m, s * D:(s + 1) * D].rearrange("p (h r) -> p h r", r=DK),
                            bv_sb[:].rearrange("p (h r) -> p h r", r=DK), ALU.add)
                    last.then_inc(s_front_v, 1)

            def shift(g, k):
                c = k % 2
                s = score[:, 2 * c:2 * c + 2, :].rearrange("p q (h t) -> p (q h) t", t=TOK)
                wait(dve, s_score, g * 16 + 2 * k + 2)
                nc.vector.reduce_max(row_max[:, c, :], s, AX.X).then_inc(s_max, 1)
                wait(dve, s_max, g * 8 + k + 1)
                wait(dve, s_swap, g * 16 + 2 * k - 2)
                nc.vector.tensor_tensor(probs[:, c], s, row_max[:, c, :].unsqueeze(2).broadcast_to([P, 8, TOK]),
                                        ALU.subtract).then_inc(s_shift, 1)

            def divide_by_sums(i):
                heads = work[:, 0, :].rearrange("p (h r) -> p h r", r=32)
                wait(dve, s_back, i + 1)
                nc.vector.reciprocal(inv_sum[:], heads[:, :, DK]).then_inc(s_inv, 1)
                wait(dve, s_inv, i + 1)
                nc.vector.tensor_tensor(attn[:].rearrange("p (h r) -> p h r", r=DK), heads[:, :, 0:DK],
                                        inv_sum[:].unsqueeze(2).broadcast_to([P, HEADS, DK]), ALU.mult).then_inc(s_attn, 1)

            def add_residual(i, b, u):
                wait(dve, s_proj, i + 1)
                nc.vector.tensor_tensor(x1[:, b, :], work[:, 1, 0:D], x_bo[:, u, b, :], ALU.add).then_inc(s_x1, 1)

            def route_shift(g):
                steps = Steps(dve, s_route, g * ROUTE_STEPS, LN_STEPS)
                wait(dve, s_logit, g + 1)
                raw = work[:, 0, 0:GROUP * EXPERTS].rearrange("p (s e) -> p s e", e=EXPERTS)
                steps.then(nc.vector.reduce_max(best[:], raw, AX.X))
                steps.done(nc.vector.tensor_tensor(logits[:], raw, over_experts(best[:]), ALU.subtract))
                assert steps.n == SHIFTED

            def route_choose(g):
                steps = Steps(dve, s_route, g * ROUTE_STEPS, SHIFTED)
                wait(dve, s_lexp, g + 1)
                steps.then(nc.vector.reduce_sum(total[:], prob[:], AX.X))
                steps.then(nc.vector.reciprocal(share[:], total[:]))
                steps.then(nc.vector.tensor_tensor(prob[:], prob[:], over_experts(share[:]), ALU.mult))
                first_best(steps, prob, top1, pick1, xn2[:, :, RANKS])
                steps.then(nc.vector.scalar_tensor_tensor(rest[:], pick1[:], -2.0, prob[:], ALU.mult, ALU.add))
                first_best(steps, rest, top2, pick2, xn2[:, :, RANKS + 1])
                steps.done(nc.vector.tensor_tensor(gap[:], top2[:], top1[:], ALU.subtract))
                assert steps.n == GAP
                steps.done(nc.vector.tensor_tensor(chosen[:], pick1[:], pick2[:], ALU.add))
                steps.then(nc.vector.tensor_tensor(chosen_f[:], pick1[:], pick2[:], ALU.add))
                for b in range(GROUP):
                    steps.then(nc.vector.tensor_tensor(seen[:, b + 1, :], seen[:, b, :], chosen_f[:, b, :], ALU.add))
                steps.then(nc.vector.tensor_copy(seen_bf[:], seen[:]))
                assert steps.n == CHOSEN
                steps.done(nc.vector.tensor_copy(seen[:, 0, :], seen[:, GROUP, :]))
                return steps.n

            def route_place(g, n):
                steps = Steps(dve, s_route, g * ROUTE_STEPS, n)
                wait(dve, s_place, g + 1)
                steps.then(nc.vector.tensor_tensor(place[:], work[:, 1, 0:GROUP * EXPERTS].rearrange("p (s e) -> p s e", e=EXPERTS),
                                                   over_group(region_base), ALU.add))
                assert steps.n == PLACES_READ, steps.n
                for k, pick in enumerate((pick1, pick2)):
                    steps.then(nc.vector.tensor_tensor(picked[:], pick[:], place[:], ALU.mult))
                    steps.then(nc.vector.reduce_sum(slot_f[:, k * GROUP:(k + 1) * GROUP], picked[:], AX.X))
                wait(dve, s_gexp, g + 1)
                w1, w2 = (xn2[:, :, WEIGHTS + k] for k in range(2))
                steps.then(nc.vector.tensor_scalar(total[:], gap[:], 1.0, None, ALU.add))
                steps.then(nc.vector.reciprocal(w1, total[:]))
                steps.done(nc.vector.tensor_tensor(w2, gap[:], w1, ALU.mult))
                steps.done(nc.vector.tensor_scalar(xn2[:, :, TOKEN], xn2[:, :, TOKEN], float(GROUP * TOK), None, ALU.add))
                if not isinstance(g, int) or g > 0:
                    wait(dve, s_scat, BLANKS * 16 + g * 2 * GROUP * 16)
                steps.done(nc.vector.tensor_copy(slots_now[:], slot_f[:]))
                assert steps.n == ROUTE_STEPS, steps.n

            rounds = iter([0, 1, 0, 1, 0, 1, 0, 1])

            def stage_a(g, core, prev, prev2, nxt, far):
                u = next(rounds)
                old = (g - 1) * GROUP
                for k in range(8):
                    if core:
                        shift(g, k)
                    if k in (0, 2, 4) and prev:
                        b = k // 2 + 1
                        add_residual(old + b, b, 1 - u)
                        if b < 3:
                            divide_by_sums(old + b + 1)
                    if k == 4 and core:
                        divide_by_sums(g * GROUP)
                    if k == 6 and core:
                        if prev:
                            wait(dve, s_res, g * 16)
                        add_residual(g * GROUP, 0, u)
                        divide_by_sums(g * GROUP + 1)
                    if k == 0 and core:
                        copy_values(g)
                    if k == 1 and nxt:
                        first_norm_stats(g + 1)
                    if k == 1 and prev2:
                        route_shift(g - 2)
                    if k == 2 and nxt:
                        first_norm(g + 1)
                    if k == 2 and prev2:
                        chosen_at = route_choose(g - 2)
                    if k == 3 and nxt:
                        copy_normed(g + 1)
                    if k == 3 and prev2:
                        route_place(g - 2, chosen_at)
                    if k == 4 and nxt:
                        copy_keys(g + 1)
                    if k == 4 and prev:
                        wait(dve, s_x1, g * GROUP)
                        norm_stats(Steps(dve, s_route, (g - 1) * ROUTE_STEPS), x1, var_eps2)
                    if k == 5 and nxt:
                        copy_queries(g + 1, 1 - u)
                    if k == 5 and prev:
                        wait(dve, s_rstd2, g)
                        wait(dve, s_scat, BLANKS * 16 + (g - 1) * 2 * GROUP * 16)
                        normalise(xn2, x1, rstd2, s_norm2)
                    if k == 6 and prev:
                        wait(dve, s_n2T, (g - 1) * 2 + 1)
                        nc.vector.tensor_copy(xn2T[:, 0, :], work[:, 0, :]).then_inc(s_n2Tv, 1)

            dve.wait_ge(s_bias, 64)
            dve.wait_ge(s_const, 10)
            dve.wait_ge(s_masks, 5)
            first_norm_stats(0)
            first_norm(0)
            copy_normed(0)
            copy_keys(0)
            copy_queries(0, 0)
            run_stage_a(dve, stage_a)

            steps = Steps(dve, s_table)
            dve.wait_ge(s_count, 1)
            steps.then(nc.vector.tensor_tensor(count[:], work[:, 0, 0:EXPERTS], blank[:, 0:EXPERTS], ALU.add))
            steps.then(nc.vector.scalar_tensor_tensor(pad_f[:], count[:], lane[:, 0:1], region_base[:], ALU.add, ALU.add))
            steps.then(nc.vector.tensor_copy(pad_rows[:], pad_f[:]))
            assert steps.n == PADS_MADE
            m = TOKENS // P
            dve.wait_ge(s_const, 11)
            steps.then(nc.vector.tensor_tensor(over, count[:].unsqueeze(2).broadcast_to([P, EXPERTS, m]), edges, ALU.is_gt))
            steps.then(nc.vector.reduce_sum(n_tiles[:], over, AX.X))
            steps.then(nc.vector.tensor_copy(tiles_to[:], n_tiles[:]))
            for e in range(1, EXPERTS):
                steps.then(nc.vector.tensor_tensor(tiles_to[:, e:e + 1], tiles_to[:, e - 1:e], n_tiles[:, e:e + 1], ALU.add))
            by_expert = [P, TABLE, EXPERTS]
            steps.then(nc.vector.tensor_tensor(past, tiles_to[:].unsqueeze(1).broadcast_to(by_expert),
                                               tile_no[:].unsqueeze(2).broadcast_to(by_expert), ALU.is_le))
            steps.then(nc.vector.reduce_sum(expert_f[:], past, AX.X))
            steps.then(nc.vector.tensor_tensor(past_tiles, past, n_tiles[:].unsqueeze(1).broadcast_to(by_expert), ALU.mult))
            steps.then(nc.vector.reduce_sum(skipped[:], past_tiles, AX.X))
            steps.then(nc.vector.tensor_tensor(row_f[:], tile_no[:], skipped[:], ALU.subtract))
            steps.then(nc.vector.tensor_scalar(skipped[:], expert_f[:], float(REGION), None, ALU.mult))
            steps.then(nc.vector.scalar_tensor_tensor(row_f[:], row_f[:], float(P), skipped[:], ALU.mult, ALU.add))
            steps.then(nc.vector.tensor_copy(row_table[:], row_f[0:1]))
            steps.then(nc.vector.tensor_scalar(expert_f[:], expert_f[:], float(EXPERTS - 1), None, ALU.min))
            steps.then(nc.vector.tensor_copy(expert_table[:], expert_f[0:1]))
            steps.then(nc.vector.tensor_scalar(tile_rank[:], expert_f[:], -1.0, float(EXPERTS), ALU.mult, ALU.add))
            assert steps.n == TABLE_STEPS, steps.n

            def copy_tileT(t, u):
                dve.wait_ge(s_xt, t + 1)
                nc.vector.tensor_copy(xsT[:, u, :], swap[:, 0:DC * P]).then_inc(s_xtc, 1)

            def fuse(t, u):
                dve.wait_ge(s_silu, t + 1)
                dve.wait_ge(s_up, t + 1)
                nc.vector.tensor_tensor(fused[:, u, :], gated[:, u, :], score[:, 2 + u, :], ALU.mult).then_inc(s_fuse, 1)

            def read_rows_ends(t, u, v, loads):
                dve.wait_ge(s_xs[u], loads * 16)
                nc.vector.scalar_tensor_tensor(pair[:], xs[:, u, RANKS:RANKS + 2], tile_rank[:, bass.ds(t, 1)],
                                               xs[:, u, WEIGHTS:WEIGHTS + 2], ALU.is_equal, ALU.mult).then_inc(s_pair, 1)
                nc.vector.tensor_copy(token[:, v, :], xs[:, u, TOKEN:ROW])
                dve.wait_ge(s_pair, t + 1)
                nc.vector.reduce_sum(weight[:, v, :], pair[:], AX.X).then_inc(s_meta, 1)

            def copy_y(t, u, v):
                dve.wait_ge(s_down, t + 1)
                nc.vector.tensor_scalar(ys[:, u, :], work[:, u, 0:D], weight[:, v, :], None, ALU.mult).then_inc(s_y, 1)

            copy_tileT(0, 0)
            read_rows_ends(0, 0, 0, 1)
            copy_tileT(1, 1)
            dve.wait_ge(s_meta, 1)
            read_rows_ends(1, 1, 1, 1)
            fuse(0, 0)

            def expert_tiles(tt, first):
                for v in range(4):
                    t, u = tt * 4 + v + 1, (1 + v) % 2
                    fuse(t, u)
                    copy_tileT(t + 1, 1 - u)
                    dve.wait_ge(s_meta, t + 1)
                    if not first or v > 1:
                        dve.wait_ge(s_acc, (t - 2) * 16)
                    read_rows_ends(t + 1, 1 - u, (v + 2) % 4, tt * 2 + v // 2 + 2)
                    copy_y(t - 1, 1 - u, v)

            expert_tiles(0, True)
            with dve.Fori(1, (TILES - 1) // 4) as tt:
                expert_tiles(tt, False)
            dve.wait_ge(s_acc, (TILES - 2) * 16)
            copy_y(TILES - 1, 0, 0)


_INS = ['x', 'ctx_1024', 'L0_xattn_Wq', 'L0_xattn_bq', 'L0_xattn_Wk', 'L0_xattn_bk', 'L0_xattn_Wv', 'L0_xattn_bv',
        'L0_xattn_Wo', 'L0_xattn_bo', 'L0_ffn_kernel_router_DE', 'L0_ffn_kernel_gating_EDF',
        'L0_ffn_kernel_up_EDF', 'L0_ffn_kernel_down_EFD']


def kernel(**inputs):
    import numpy as _np
    import concourse.bacc as _bacc
    from concourse.bass_utils import run_bass_kernel_spmd as _run

    nc = _bacc.Bacc("TRN2", target_bir_lowering=False, num_devices=1)
    arrays, args = {}, []
    for name in _INS:
        a = _np.asarray(inputs[name])
        if name == 'ctx_1024':
            a = a.reshape(TOKENS, D).T
        a = _np.ascontiguousarray(a)
        arrays[f"in_{name}"] = a
        args.append(nc.dram_tensor(f"in_{name}", a.shape, mybir.dt.from_np(a.dtype), kind="ExternalInput").ap())
    out = nc.dram_tensor("out_0", (TOKENS + P, D), mybir.dt.float32, kind="ExternalOutput").ap()
    moe_attention(nc, *args, out)
    r = _run(nc, [arrays], core_ids=[0])
    return r.results[0]["out_0"][:TOKENS].reshape(SEQS, TOK, D)
```

```python
from contextlib import ExitStack

import concourse.bass as bass
from concourse import mybir

P = 128
SEQS, TOK, D = 64, 128, 256
HEADS, DK = 16, 16
EXPERTS, F = 8, 512
GROUP = 4
GROUPS = SEQS // GROUP
DC = D // P
FC = F // P
QUADS = HEADS // 4
TOKENS = SEQS * TOK
REGION = TOKENS + P
USED_TILES = 2 * TOKENS // P + EXPERTS - 1
TILES = USED_TILES
STEPS, REST = divmod(TILES - 1, 4)
assert TILES % 2 == 1
TABLE = TILES + 1
SPARE_TILES = TABLE - 2 * TOKENS // P
SPARE = EXPERTS * REGION
SORTED_ROWS = SPARE + SPARE_TILES * P
EPS = 1e-5
WEIGHTS, RANKS, TOKEN, ROW = D, D + 2, D + 4, D + 5
BLANKS = SPARE_TILES + 1


class Steps:

    def __init__(self, eng, sem, base=0, n=0):
        self.eng, self.sem, self.base, self.n = eng, sem, base, n

    def done(self, instruction):
        self.n += 1
        instruction.then_inc(self.sem, 1)

    def wait(self):
        self.eng.wait_ge(self.sem, self.base + self.n)

    def then(self, instruction):
        self.done(instruction)
        self.wait()


def moe_attention(nc, x, ctxT, wq, bq, wk, bk, wv, bv, wo, bo, router, gating, up, down, out):
    fp32, bf16 = mybir.dt.float32, mybir.dt.bfloat16
    u32, i32 = mybir.dt.uint32, mybir.dt.int32
    ACT, ALU, AX = mybir.ActivationFunctionType, mybir.AluOpType, mybir.AxisListType

    with ExitStack() as ctx:
        def sb(name, shape, dt=fp32):
            return ctx.enter_context(nc.sbuf_tensor(name, shape, dt))

        def sem(name):
            return ctx.enter_context(nc.semaphore(name))

        sorted_x = nc.dram_tensor("sorted_x", (SORTED_ROWS, ROW), fp32, kind="Internal").ap()

        wq_sb, wk_sb, wv_sb = (sb(n, [P, DC, D]) for n in ("wq_sb", "wk_sb", "wv_sb"))
        wo_sb = sb("wo_sb", [P, DC, D])
        wr_sb = sb("wr_sb", [P, DC, 32])
        bq_sb, bk_sb = sb("bq_sb", [P, DC]), sb("bk_sb", [P, DC])
        bv_sb, bo_sb = sb("bv_sb", [P, D]), sb("bo_sb", [P, D])
        gate_sb = sb("gate_sb", [P, EXPERTS * DC * F])
        up_sb = sb("up_sb", [P, EXPERTS * DC * F])
        down_sb = sb("down_sb", [P, EXPERTS * FC * D])
        ident = sb("ident", [P, P])
        before = sb("before", [P, P], bf16)
        ones = sb("ones", [P, P], bf16)
        head_rows = sb("head_rows", [P, 8])
        tile_rows = sb("tile_rows", [P, 4])
        minus_half = sb("minus_half", [P, GROUP])
        region_base = sb("region_base", [P, EXPERTS])
        first_rank = sb("first_rank", [P, EXPERTS])
        blank = sb("blank", [P, ROW])

        x_sb = sb("x_sb", [P, GROUP, D])
        x_bo = sb("x_bo", [P, 2, GROUP, D])
        ctxT_sb = sb("ctxT_sb", [P, DC, GROUP * TOK])
        stats = sb("stats", [P, GROUP, 6])
        mean_var = sb("mean_var", [P, GROUP, 2])
        var_eps, var_eps2, rstd, rstd2 = (sb(n, [P, GROUP]) for n in ("var_eps", "var_eps2", "rstd", "rstd2"))
        xn = sb("xn", [P, GROUP, D])
        xnT = sb("xnT", [P, DC, GROUP * TOK])
        qT = sb("qT", [P, 2, DC, GROUP * TOK])
        kT = sb("kT", [P, DC, GROUP * TOK])
        k_blocks = sb("k_blocks", [P, 2, DC, 4 * TOK])
        v_aug = sb("v_aug", [P, GROUP, HEADS, 32])
        row_max = sb("row_max", [P, 2, 8])
        probs = sb("probs", [P, 2, 8, TOK])
        probsT = sb("probsT", [P, 2, 4 * TOK])
        attT = sb("attT", [P, QUADS * TOK])
        inv_sum = sb("inv_sum", [P, HEADS])
        attn = sb("attn", [P, D])
        attnT = sb("attnT", [P, D])
        x1 = sb("x1", [P, GROUP, D])
        xn2 = sb("xn2", [P, GROUP, ROW])
        xn2T = xnT
        GE = [P, GROUP, EXPERTS]
        logits, prob, tied, rest, pick1, pick2, place, picked = (
            sb(n, GE) for n in ("logits", "prob", "tied", "rest", "pick1", "pick2", "place", "picked"))
        best, total, top1, top2, gap, share = (
            sb(n, [P, GROUP]) for n in ("best", "total", "top1", "top2", "gap", "share"))
        logitsT = sb("logitsT", [P, TOK])
        chosen = sb("chosen", GE, bf16)
        chosen_f = sb("chosen_f", GE)
        seen = sb("seen", [P, GROUP + 1, EXPERTS])
        seen_bf = sb("seen_bf", [P, GROUP + 1, EXPERTS], bf16)
        slot_f = sb("slot_f", [P, 2 * GROUP])
        slots_now = sb("slots_now", [P, 2 * GROUP], u32)

        lane = sb("lane", [P, 1])
        count = sb("count", [P, EXPERTS])
        pad_f = sb("pad_f", [P, EXPERTS])
        pad_rows = sb("pad_rows", [P, EXPERTS], u32)
        tile_no = sb("tile_no", [P, TABLE])
        n_tiles = sb("n_tiles", [P, EXPERTS])
        tiles_to = sb("tiles_to", [P, EXPERTS])
        rooms = (k_blocks[:].rearrange("p u c t -> p (u c t)"), v_aug[:].rearrange("p s h r -> p (s h r)"))
        past, past_tiles = (room[:, 0:TABLE * EXPERTS].rearrange("p (a b) -> p a b", b=EXPERTS) for room in rooms)
        over, edges = (room[:, TABLE * EXPERTS:TABLE * EXPERTS + EXPERTS * (TOKENS // P)].rearrange(
            "p (e m) -> p e m", e=EXPERTS) for room in rooms)
        expert_f, skipped, row_f = (sb(n, [P, TABLE]) for n in ("expert_f", "skipped", "row_f"))
        tile_rank = sb("tile_rank", [P, TABLE])
        row_table = sb("row_table", [1, TABLE], i32)
        expert_table = sb("expert_table", [1, TABLE], i32)

        xs = x_bo[:].rearrange("p u s d -> p u (s d)")[:, :, 0:ROW]
        xsT = xnT[:, :, 0:DC * P]
        gated, fused = qT[:, 0], kT
        fusedT = probs[:].rearrange("p u h t -> p u (h t)")[:, :, 0:F]
        ys = xn[:, 0:2, :]
        pair = sb("pair", [P, 2])
        weight = sb("weight", [P, 4, 1])
        token = sb("token", [P, 4, 1], u32)

        score = ctx.enter_context(nc.psum_tensor("score", [P, 4, 512], fp32))
        swap = ctx.enter_context(nc.psum_tensor("swap", [P, 512], fp32))
        att = ctx.enter_context(nc.psum_tensor("att", [P, 512], fp32))
        work = ctx.enter_context(nc.psum_tensor("work", [P, 2, 512], fp32))

        s_wkvq, s_bias, s_wo, s_experts = (sem(n) for n in ("wkvq_loaded", "bias_loaded", "wo_loaded", "experts_loaded"))
        s_x, s_ctx, s_xbo = sem("x_loaded"), sem("ctx_loaded"), sem("x_bo_ready")
        s_kb = sem("keys_placed")
        s_res, s_scat, s_pad = (sem(n) for n in ("resid_stored", "rows_written", "pads_written"))
        s_zero, s_masks, s_const = (sem(n) for n in ("zeroed", "masks_ready", "consts_ready"))
        s_ln, s_rstd, s_norm = (sem(n) for n in ("ln1_steps", "rstd_ready", "x_normed"))
        s_front, s_front_v, s_front_a = (sem(n) for n in ("front_product", "front_copied_by_vector", "front_copied_by_scalar"))
        s_score, s_max, s_shift, s_exp = (sem(n) for n in ("scores_ready", "row_max_ready", "scores_shifted", "probs_ready"))
        s_swap, s_probsT, s_att, s_attT = (sem(n) for n in ("probs_swapped", "probsT_ready", "att_product", "attT_ready"))
        s_back, s_inv, s_attn = (sem(n) for n in ("att_swapped_back", "inverse_sums_ready", "attn_normalised"))
        s_fwd, s_attnT = sem("attn_swapped"), sem("attnT_ready")
        s_proj, s_x1 = sem("projected"), sem("x1_ready")
        s_rstd2, s_norm2 = sem("rstd2_ready"), sem("x1_normed")
        s_n2T, s_n2Tv, s_n2Ta = (sem(n) for n in ("x1_swapped", "x1T_copied_by_vector", "x1T_copied_by_scalar"))
        s_logitT, s_logitTc = sem("logits_by_expert"), sem("logits_by_expert_copied")
        s_logit, s_route, s_lexp, s_gexp = (sem(n) for n in ("logits_ready", "route_steps", "router_exp_ready", "gap_exp_ready"))
        s_place = sem("places_ready")
        s_count, s_table = sem("counts_ready"), sem("table_steps")
        s_xs = [sem("tile_loaded_0"), sem("tile_loaded_1")]
        s_pair, s_meta, s_acc = sem("row_weights_masked"), sem("row_weights_ready"), sem("tile_added")
        s_xt, s_xtc, s_gate, s_up, s_silu, s_fuse = (sem(n) for n in (
            "tile_swapped", "tileT_ready", "gate_product", "up_product", "silu_ready", "fused_ready"))
        s_ft, s_ftc, s_down, s_y = (sem(n) for n in ("fused_swapped", "fusedT_ready", "down_product", "y_ready"))

        LN_STEPS = 3
        ROUTE_STEPS = 38
        SHIFTED = 5
        GAP = 20
        CHOSEN = 27
        PLACES_READ = 33
        TABLE_STEPS = 24
        PADS_MADE = 3

        block = ctx.enter_context(nc.Block())

        def wait(eng, semaphore, value):
            if not isinstance(value, int) or value > 0:
                eng.wait_ge(semaphore, value)

        def run_stage_a(eng, group):
            def at(g):
                group(g, g < GROUPS, 1 <= g <= GROUPS, g >= 2, g + 1 < GROUPS, g + 2 < GROUPS)

            at(0)
            at(1)
            with eng.Fori(1, GROUPS // 2 - 1) as pair:
                for u in range(2):
                    group(pair * 2 + u, True, True, True, True, True)
            for g in range(GROUPS - 2, GROUPS + 2):
                at(g)

        @block.sync
        def _(sp):
            def load_x(g):
                sp.dma_start(x_sb[:], x[bass.ds(g * GROUP, GROUP)].rearrange("s t d -> t s d")).then_inc(s_x, 16)

            def load_ctx(g):
                sp.dma_start(ctxT_sb[:], ctxT[:, bass.ds(g * GROUP * TOK, GROUP * TOK)].rearrange(
                    "(c p) t -> p c t", p=P)).then_inc(s_ctx, 16)

            load_x(0)
            load_ctx(0)
            for w_sb, w in ((wk_sb, wk), (wv_sb, wv), (wq_sb, wq)):
                sp.dma_start(w_sb[:], w.rearrange("(c p) n -> p c n", p=P)).then_inc(s_wkvq, 16)
            for b_sb, b in ((bk_sb, bk), (bq_sb, bq)):
                sp.dma_start(b_sb[:], b.rearrange("(c p) -> p c", p=P), allow_slow_non_contiguous=True).then_inc(s_bias, 16)
            for b_sb, b in ((bv_sb, bv), (bo_sb, bo)):
                sp.dma_start(b_sb[:], b.partition_broadcast(P)).then_inc(s_bias, 16)
            sp.dma_start(wo_sb[:], wo.rearrange("(c p) n -> p c n", p=P)).then_inc(s_wo, 16)
            sp.wait_ge(s_zero, 1)
            sp.dma_start(wr_sb[:, :, 0:EXPERTS], router.rearrange("(c p) e -> p c e", p=P)).then_inc(s_wo, 16)
            for e in range(EXPERTS):
                for w_sb, w, c in ((gate_sb, gating, DC), (up_sb, up, DC), (down_sb, down, FC)):
                    n = w_sb.shape[1] // EXPERTS
                    sp.dma_start(w_sb[:, e * n:(e + 1) * n].rearrange("p (c f) -> p c f", c=c),
                                 w[e].rearrange("(c p) f -> p c f", p=P)).then_inc(s_experts, 16)
            sp.wait_ge(s_norm, 1)
            sp.wait_ge(s_xbo, 1)
            load_x(1)

            def stage_a(g, core, prev, prev2, nxt, far):
                if nxt:
                    wait(sp, s_front, g * 8 + 8)
                    load_ctx(g + 1)
                if prev:
                    wait(sp, s_x1, g * GROUP)
                    sp.dma_start(out[bass.ds((g - 1) * GROUP * TOK, GROUP * TOK)].rearrange("(s t) d -> t s d", t=TOK),
                                 x1[:]).then_inc(s_res, 16)
                if far:
                    wait(sp, s_xbo, g + 2)
                    load_x(g + 2)

            run_stage_a(sp, stage_a)

            sp.wait_ge(s_table, TABLE_STEPS)
            sp.wait_ge(s_scat, BLANKS * 16 + GROUPS * 2 * GROUP * 16)
            sp.wait_ge(s_pad, EXPERTS * 16)

            def row_of(t):
                return sp.value_load(row_table[0:1, bass.ds(t, 1)], min_val=0, max_val=SORTED_ROWS - P)

            def load_tile(t, u):
                sp.dma_start(xs[:, u, :], sorted_x[bass.ds(row_of(t), P), :]).then_inc(s_xs[u], 16)

            load_tile(0, 0)
            load_tile(1, 1)
            with sp.Fori(0, (TILES - 1) // 2) as tt:
                for u in range(2):
                    t = tt * 2 + u
                    sp.wait_ge(s_xt, t + 1)
                    sp.wait_ge(s_meta, t + 1)
                    load_tile(t + 2, u)

        @block.gpsimd
        def _(pool):
            nc.gpsimd.memset(wr_sb[:], 0.0).then_inc(s_zero, 1)
            nc.gpsimd.memset(head_rows[:], 1.0).then_inc(s_zero, 1)
            nc.gpsimd.memset(ident[:], 0.0).then_inc(s_zero, 1)
            nc.gpsimd.memset(before[:], 1.0).then_inc(s_zero, 1)
            nc.gpsimd.memset(v_aug[:], 0.0).then_inc(s_zero, 1)
            pool.wait_ge(s_zero, 5)
            nc.gpsimd.affine_select(out=ident[:], in_=ident[:], compare_op=ALU.not_equal, fill=1.0, base=0,
                                    pattern=[[-1, P]], channel_multiplier=1).then_inc(s_masks, 1)
            nc.gpsimd.affine_select(out=before[:], in_=before[:], compare_op=ALU.is_gt, fill=0.0, base=0,
                                    pattern=[[1, P]], channel_multiplier=-1).then_inc(s_masks, 1)
            nc.gpsimd.memset(v_aug[:, :, :, DK:DK + 1], 1.0).then_inc(s_masks, 1)
            nc.gpsimd.affine_select(out=head_rows[:], in_=head_rows[:], compare_op=ALU.is_ge, fill=0.0, base=0,
                                    pattern=[[-DK, 8]], channel_multiplier=1).then_inc(s_masks, 1)
            pool.wait_ge(s_masks, 4)
            nc.gpsimd.affine_select(out=head_rows[:], in_=head_rows[:], compare_op=ALU.is_gt, fill=0.0, base=DK,
                                    pattern=[[DK, 8]], channel_multiplier=-1).then_inc(s_masks, 1)
            nc.gpsimd.memset(minus_half[:], -0.5).then_inc(s_const, 1)
            nc.gpsimd.memset(ones[:], 1.0).then_inc(s_const, 1)
            nc.gpsimd.memset(blank[:, 0:TOKEN], 0.0).then_inc(s_const, 1)
            nc.gpsimd.memset(seen[:], 0.0).then_inc(s_const, 1)
            small = dict(allow_small_or_imprecise_dtypes=True)
            nc.gpsimd.iota(region_base[:], pattern=[[REGION, EXPERTS]], base=0, channel_multiplier=0, **small).then_inc(s_const, 1)
            nc.gpsimd.iota(first_rank[:], pattern=[[-1, EXPERTS]], base=EXPERTS, channel_multiplier=0, **small).then_inc(s_const, 1)
            nc.gpsimd.iota(lane[:], pattern=[[0, 1]], base=0, channel_multiplier=1, **small).then_inc(s_const, 1)
            nc.gpsimd.iota(tile_no[:], pattern=[[1, TABLE]], base=0, channel_multiplier=0, **small).then_inc(s_const, 1)
            nc.gpsimd.iota(blank[:, TOKEN:ROW], pattern=[[0, 1]], base=TOKENS, channel_multiplier=1, **small).then_inc(s_const, 1)
            nc.gpsimd.iota(xn2[:, :, TOKEN], pattern=[[TOK, GROUP]], base=-GROUP * TOK, channel_multiplier=1, **small).then_inc(s_const, 1)
            pool.wait_ge(s_masks, 5)
            nc.gpsimd.tensor_tensor(tile_rows[:], head_rows[:, 0:4], head_rows[:, 4:8], ALU.add).then_inc(s_const, 1)
            pool.wait_ge(s_const, 11)
            def place_keys(g, b):
                wait(pool, s_score, g * 8 + 2 * b - 2)
                for c in range(DC):
                    nc.gpsimd.tensor_tensor(
                        k_blocks[:, b % 2, c, :].rearrange("p (h t) -> p h t", t=TOK),
                        kT[:, c, b * TOK:(b + 1) * TOK].unsqueeze(1).broadcast_to([P, 4, TOK]),
                        tile_rows[:].unsqueeze(2).broadcast_to([P, 4, TOK]), ALU.mult).then_inc(s_kb, 1)

            def root(g):
                wait(pool, s_ln, g * LN_STEPS + LN_STEPS)
                nc.gpsimd.tensor_tensor(rstd[:], var_eps[:], minus_half[:], ALU.pow).then_inc(s_rstd, 1)

            def keep_x(g, u, first):
                wait(pool, s_norm, g + 1)
                if not first:
                    wait(pool, s_x1, (g - 1) * GROUP)
                nc.gpsimd.tensor_tensor(x_bo[:, u], x_sb[:], bo_sb[:].unsqueeze(1).broadcast_to([P, GROUP, D]),
                                        ALU.add).then_inc(s_xbo, 1)

            def first_keys(g):
                wait(pool, s_front_v, g * 4 + 1)
                wait(pool, s_front_a, g * 4 + 3)
                place_keys(g, 0)
                place_keys(g, 1)

            rounds = iter([0, 1, 0, 1, 0, 1, 0, 1])

            def stage_a(g, core, prev, prev2, nxt, far):
                u = next(rounds)
                if core:
                    place_keys(g, 2)
                if nxt:
                    root(g + 1)
                if core:
                    place_keys(g, 3)
                if nxt:
                    keep_x(g + 1, 1 - u, False)
                if prev2:
                    wait(pool, s_route, (g - 2) * ROUTE_STEPS + ROUTE_STEPS)
                    pool.nop(nofuse=True)
                    for i in range(2 * GROUP):
                        pool.indirect_dma_start(
                            out=sorted_x[:, :], out_offset=bass.IndirectOffsetOnAxis(ap=slots_now[:, i:i + 1], axis=0),
                            in_=xn2[:, i % GROUP, :], in_offset=None).then_inc(s_scat, 16)
                if prev:
                    wait(pool, s_route, (g - 1) * ROUTE_STEPS + LN_STEPS)
                    nc.gpsimd.tensor_tensor(rstd2[:], var_eps2[:], minus_half[:], ALU.pow).then_inc(s_rstd2, 1)
                if nxt:
                    first_keys(g + 1)

            pool.wait_ge(s_bias, 64)
            root(0)
            keep_x(0, 0, True)
            first_keys(0)
            for i in range(SPARE_TILES):
                pool.dma_start(sorted_x[SPARE + i * P:SPARE + (i + 1) * P, :], blank[:]).then_inc(s_scat, 16)
            pool.dma_start(out[TOKENS:TOKENS + P, :], blank[:, 0:D]).then_inc(s_scat, 16)
            run_stage_a(pool, stage_a)
            small = dict(allow_small_or_imprecise_dtypes=True)
            nc.gpsimd.iota(edges, pattern=[[0, EXPERTS], [P, TOKENS // P]], base=0, channel_multiplier=0, **small).then_inc(s_const, 1)
            pool.wait_ge(s_table, PADS_MADE)
            for e in range(EXPERTS):
                pool.indirect_dma_start(
                    out=sorted_x[:, :], out_offset=bass.IndirectOffsetOnAxis(ap=pad_rows[:, e:e + 1], axis=0),
                    in_=blank[:], in_offset=None).then_inc(s_pad, 16)

            pool.wait_ge(s_res, GROUPS * 16)
            pool.wait_ge(s_scat, BLANKS * 16)

            def add_tile(t, u, v):
                pool.wait_ge(s_y, t + 1)
                pool.nop(nofuse=True)
                pool.indirect_dma_start(
                    out=out[:, :], out_offset=bass.IndirectOffsetOnAxis(ap=token[:, v, :], axis=0),
                    in_=ys[:, u, :], in_offset=None, compute_op=ALU.add).then_inc(s_acc, 16)

            def add_tiles(tt, n):
                for v in range(n):
                    t = tt * 4 + v + 1
                    pool.wait_ge(s_acc, t * 16)
                    add_tile(t, (v + 1) % 2, (v + 1) % 4)

            add_tile(0, 0, 0)
            with pool.Fori(0, STEPS) as tt:
                add_tiles(tt, 4)
            add_tiles(STEPS, REST)
            pool.wait_ge(s_acc, TILES * 16)

        @block.tensor
        def _(pe):
            def product(dst, pairs):
                for i, (lhsT, rhs) in enumerate(pairs):
                    last = nc.tensor.matmul(dst, lhsT, rhs, start=(i == 0), stop=(i == len(pairs) - 1))
                return last

            banks = {"qT": iter([0, 1, 0, 1, 0, 1, 0, 1])}

            def norm_swapped(g, c):
                wait(pe, s_norm, g + 1)
                if c == 1:
                    wait(pe, s_front_a, g * 4 + 1)
                for b in range(GROUP):
                    last = nc.tensor.transpose(work[:, 0, b * P:(b + 1) * P], xn[:, b, c * P:(c + 1) * P], ident[:])
                last.then_inc(s_front, 1)

            def keys(g, m):
                wait(pe, s_ctx, g * 16 + 16)
                product(work[:, m, :], [(wk_sb[:, c, m * P:(m + 1) * P], ctxT_sb[:, c, :]) for c in range(DC)]).then_inc(s_front, 1)

            def queries(g, m):
                wait(pe, s_front_v, g * 4 + 1 + m)
                wait(pe, s_front_a, g * 4 + 2)
                product(work[:, 0, :], [(wq_sb[:, c, m * P:(m + 1) * P], xnT[:, c, :]) for c in range(DC)]).then_inc(s_front, 1)

            def values(g, m):
                for s in range(2):
                    t = (2 * m + s) * TOK
                    last = product(work[:, m, s * D:(s + 1) * D], [(ctxT_sb[:, c, t:t + TOK], wv_sb[:, c, :]) for c in range(DC)])
                last.then_inc(s_front, 1)

            def scores(g, u, k):
                b, c = k // 2, k % 2
                if k == 0:
                    wait(pe, s_front_v, g * 4 + 2)
                    wait(pe, s_front_a, g * 4 + 4)
                wait(pe, s_shift, g * 8 + k - 1)
                wait(pe, s_kb, g * 8 + k + 1)
                for q in range(2):
                    rows = slice(64 * q, 64 * q + 64)
                    last = nc.tensor.matmul(score[:, 2 * c + q, :], qT[rows, u, c, b * TOK:(b + 1) * TOK],
                                            k_blocks[rows, b % 2, c, :], start=True, stop=True)
                last.then_inc(s_score, 1)

            def swap_probs(g, n):
                c = n // 2 % 2
                wait(pe, s_exp, g * 8 + n // 2 + 1)
                wait(pe, s_probsT, g * 16 + n)
                for j in range(4):
                    last = nc.tensor.transpose(swap[:, j * TOK:(j + 1) * TOK], probs[:, c, 4 * (n % 2) + j, :], ident[:])
                last.then_inc(s_swap, 1)

            def attend(g, n):
                b, q = n // 4, n % 4
                wait(pe, s_probsT, g * 16 + n + 1)
                if n in (0, 8):
                    wait(pe, s_front_v, g * 4 + 3 + n // 8)
                if q == 0:
                    wait(pe, s_attT, g * 4 + b)
                for j in range(4):
                    last = nc.tensor.matmul(att[32 * j:32 * j + 32, q * TOK:(q + 1) * TOK], v_aug[:, b, 4 * q + j, :],
                                            probsT[:, n % 2, j * TOK:(j + 1) * TOK], start=True, stop=True)
                last.then_inc(s_att, 1)

            def swap_back(i):
                wait(pe, s_attT, i + 1)
                wait(pe, s_attn, i)
                for q in range(QUADS):
                    last = nc.tensor.transpose(work[:, 0, q * TOK:(q + 1) * TOK], attT[:, q * TOK:(q + 1) * TOK], ident[:])
                last.then_inc(s_back, 1)

            def swap_forth(i):
                wait(pe, s_attn, i + 1)
                wait(pe, s_x1, i)
                for c in range(DC):
                    last = nc.tensor.transpose(work[:, 1, c * P:(c + 1) * P], attn[:, c * P:(c + 1) * P], ident[:])
                last.then_inc(s_fwd, 1)

            def project(i):
                wait(pe, s_attnT, i + 1)
                product(work[:, 1, 0:D], [(attnT[:, c * P:(c + 1) * P], wo_sb[:, c, :]) for c in range(DC)]).then_inc(s_proj, 1)

            def x1_swapped(g, c):
                if c == 0:
                    wait(pe, s_norm2, g + 1)
                else:
                    wait(pe, s_n2Tv, g + 1)
                for b in range(GROUP):
                    last = nc.tensor.transpose(work[:, 0, b * P:(b + 1) * P], xn2[:, b, c * P:(c + 1) * P], ident[:])
                last.then_inc(s_n2T, 1)

            def route_logits(g):
                wait(pe, s_n2Ta, g + 1)
                for c in range(DC):
                    for b in range(GROUP):
                        last = nc.tensor.matmul(work[32 * b:32 * b + 32, 0, 0:TOK], wr_sb[:, c, :],
                                                xn2T[:, c, b * TOK:(b + 1) * TOK], start=(c == 0), stop=(c == DC - 1))
                last.then_inc(s_logitT, 1)

            def swap_logits(g):
                wait(pe, s_logitTc, g + 1)
                nc.tensor.transpose(work[:, 0, 0:P], logitsT[:], ident[:]).then_inc(s_logit, 1)

            def places(g):
                wait(pe, s_route, g * ROUTE_STEPS + CHOSEN)
                for b in range(GROUP):
                    last = product(work[:, 1, b * EXPERTS:(b + 1) * EXPERTS],
                                   [(before[:], chosen[:, b, :]), (ones[:], seen_bf[:, b, :])])
                last.then_inc(s_place, 1)

            def stage_a(g, core, prev, prev2, nxt, far):
                u = next(banks["qT"])
                old = (g - 1) * GROUP
                for k in range(8):
                    if core:
                        swap_probs(g, 2 * k)
                    if k == 0 and core:
                        wait(pe, s_attn, g * GROUP - 1)
                        values(g, 0)
                        wait(pe, s_x1, g * GROUP - 2)
                        values(g, 1)
                    if core and k < 6:
                        scores(g, u, k + 2)
                    elif nxt:
                        scores(g + 1, 1 - u, k - 6)
                    if k == 1 and prev2:
                        swap_logits(g - 2)
                    if k == 4 and prev2:
                        if prev:
                            wait(pe, s_x1, g * GROUP)
                        places(g - 2)
                    if core:
                        swap_probs(g, 2 * k + 1)
                    if k == 3:
                        if nxt:
                            norm_swapped(g + 1, 1)
                        if prev:
                            project(old + 3)
                    if k == 4:
                        if nxt:
                            wait(pe, s_attn, g * GROUP + 1)
                            keys(g + 1, 0)
                        if prev2:
                            wait(pe, s_route, (g - 2) * ROUTE_STEPS + PLACES_READ)
                        if nxt:
                            wait(pe, s_x1, g * GROUP)
                            keys(g + 1, 1)
                    if k == 5 and nxt:
                        queries(g + 1, 1)
                    if k == 7 and prev:
                        x1_swapped(g - 1, 1)
                    if core:
                        attend(g, 2 * k)
                    if k == 0:
                        if prev:
                            if core:
                                wait(pe, s_front_v, g * 4 + 4)
                            swap_forth(old + 2)
                        if prev2:
                            wait(pe, s_attn, g * GROUP - 1 if prev else SEQS)
                            route_logits(g - 2)
                    if k == 1 and prev:
                        project(old + 2)
                        if prev2:
                            wait(pe, s_route, (g - 2) * ROUTE_STEPS + SHIFTED)
                        swap_back(old + 3)
                    if k == 2:
                        if prev:
                            swap_forth(old + 3)
                        if nxt:
                            wait(pe, s_attn, g * GROUP)
                            norm_swapped(g + 1, 0)
                    if k == 3 and core:
                        if nxt:
                            wait(pe, s_front_a, g * 4 + 6)
                        swap_back(g * GROUP)
                    if k == 4:
                        if nxt:
                            queries(g + 1, 0)
                        if core:
                            if nxt:
                                wait(pe, s_front_a, g * 4 + 7)
                            swap_forth(g * GROUP)
                    if k == 5 and core:
                        project(g * GROUP)
                        if nxt:
                            wait(pe, s_front_a, g * 4 + 8)
                        swap_back(g * GROUP + 1)
                    if k == 6 and core:
                        swap_forth(g * GROUP + 1)
                    if k == 7 and core:
                        project(g * GROUP + 1)
                        if prev:
                            wait(pe, s_n2Ta, g)
                        swap_back(g * GROUP + 2)
                    if core:
                        attend(g, 2 * k + 1)
                    if k == 6 and prev:
                        wait(pe, s_attn, g * GROUP + 2 if core else g * GROUP)
                        x1_swapped(g - 1, 0)

            pe.wait_ge(s_wkvq, 48)
            pe.wait_ge(s_masks, 5)
            pe.wait_ge(s_const, 8)
            pe.wait_ge(s_wo, 32)
            norm_swapped(0, 0)
            norm_swapped(0, 1)
            pe.wait_ge(s_front_a, 2)
            keys(0, 0)
            keys(0, 1)
            queries(0, 0)
            queries(0, 1)
            scores(0, 0, 0)
            scores(0, 0, 1)
            run_stage_a(pe, stage_a)
            pe.wait_ge(s_route, GROUPS * ROUTE_STEPS)
            nc.tensor.matmul(work[:, 0, 0:EXPERTS], ones[:], seen_bf[:, GROUP, :], start=True, stop=True).then_inc(s_count, 1)

            def swap_tile(t, u, loads):
                pe.wait_ge(s_xs[u], loads * 16)
                pe.wait_ge(s_xtc, t)
                for c in range(DC):
                    last = nc.tensor.transpose(swap[:, c * P:(c + 1) * P], xs[:, u, c * P:(c + 1) * P], ident[:])
                last.then_inc(s_xt, 1)

            def expert_of(t):
                return pe.value_load(expert_table[0:1, bass.ds(t, 1)], min_val=0, max_val=EXPERTS - 1)

            def gate(t, u, e):
                pe.wait_ge(s_xtc, t + 1)
                product(score[:, u, :], [(xsT[:, u, c * P:(c + 1) * P], gate_sb[:, bass.ds(e * (DC * F) + c * F, F)])
                                         for c in range(DC)]).then_inc(s_gate, 1)

            def up_(t, u, e):
                product(score[:, 2 + u, :], [(xsT[:, u, c * P:(c + 1) * P], up_sb[:, bass.ds(e * (DC * F) + c * F, F)])
                                             for c in range(DC)]).then_inc(s_up, 1)

            def swap_fused(t, u):
                pe.wait_ge(s_fuse, t + 1)
                for c in range(FC):
                    last = nc.tensor.transpose(att[:, c * P:(c + 1) * P], fused[:, u, c * P:(c + 1) * P], ident[:])
                last.then_inc(s_ft, 1)

            def down_(t, u, e):
                pe.wait_ge(s_ftc, t + 1)
                product(work[:, u, 0:D], [(fusedT[:, u, c * P:(c + 1) * P], down_sb[:, bass.ds(e * (FC * D) + c * D, D)])
                                          for c in range(FC)]).then_inc(s_down, 1)

            pe.wait_ge(s_experts, EXPERTS * 3 * 16)
            pe.wait_ge(s_table, TABLE_STEPS)
            swap_tile(0, 0, 1)
            e = expert_of(0)
            gate(0, 0, e)
            up_(0, 0, e)
            swap_tile(1, 1, 1)

            def expert_tiles(tt, n):
                for v in range(n):
                    t = tt * 4 + v + 1
                    u = (1 + v) % 2
                    e, e_last = expert_of(t), expert_of(t - 1)
                    pe.wait_ge(s_silu, t)
                    gate(t, u, e)
                    swap_fused(t - 1, 1 - u)
                    up_(t, u, e)
                    swap_tile(t + 1, 1 - u, tt * 2 + v // 2 + 2)
                    down_(t - 1, 1 - u, e_last)

            with pe.Fori(0, STEPS) as tt:
                expert_tiles(tt, 4)
            expert_tiles(STEPS, REST)
            e = expert_of(TILES - 1)
            swap_fused(TILES - 1, 0)
            down_(TILES - 1, 0, e)

        @block.scalar
        def _(act):
            def copy_normed(g, c):
                wait(act, s_front, g * 8 + 1 + c)
                nc.scalar.activation(xnT[:, c, :], work[:, 0, :], ACT.Copy).then_inc(s_front_a, 1)

            def copy_keys(g):
                wait(act, s_front, g * 8 + 4)
                wait(act, s_kb, g * 8)
                nc.scalar.activation(kT[:, 1, :], work[:, 1, :], ACT.Identity, bias=bk_sb[:, 1:2]).then_inc(s_front_a, 1)

            def copy_queries(g, u):
                wait(act, s_front, g * 8 + 6)
                nc.scalar.activation(qT[:, u, 1, :], work[:, 0, :], ACT.Identity, bias=bq_sb[:, 1:2]).then_inc(s_front_a, 1)

            def softmax_exp(g, k):
                wait(act, s_shift, g * 8 + k + 1)
                nc.scalar.activation(probs[:, k % 2], probs[:, k % 2], ACT.Exp, scale=DK ** -0.5).then_inc(s_exp, 1)

            def copy_probsT(g, n):
                wait(act, s_swap, g * 16 + n + 1)
                wait(act, s_att, g * 16 + n - 1)
                nc.scalar.activation(probsT[:, n % 2], swap[:], ACT.Copy).then_inc(s_probsT, 1)

            def copy_attT(i):
                wait(act, s_att, i * QUADS + QUADS)
                wait(act, s_back, i)
                nc.scalar.activation(attT[:], att[:], ACT.Copy).then_inc(s_attT, 1)

            def copy_attnT(i):
                wait(act, s_fwd, i + 1)
                nc.scalar.activation(attnT[:], work[:, 1, 0:D], ACT.Copy).then_inc(s_attnT, 1)

            rounds = iter([0, 1, 0, 1, 0, 1, 0, 1])

            def stage_a(g, core, prev, prev2, nxt, far):
                u = next(rounds)
                old = (g - 1) * GROUP
                for k in range(8):
                    if core:
                        softmax_exp(g, k)
                    if k == 3 and nxt:
                        copy_normed(g + 1, 0)
                    if k == 1 and prev2:
                        wait(act, s_logitT, g - 1)
                        nc.scalar.activation(logitsT[:], work[:, 0, 0:TOK], ACT.Copy).then_inc(s_logitTc, 1)
                    if k == 3 and prev2:
                        wait(act, s_route, (g - 2) * ROUTE_STEPS + GAP)
                        nc.scalar.activation(gap[:], gap[:], ACT.Exp).then_inc(s_gexp, 1)
                    if k == 0 and prev:
                        copy_attT(old + 3)
                    if k in (2, 4, 6) and core:
                        copy_attT(g * GROUP + k // 2 - 1)
                    if k in (1, 3) and prev:
                        copy_attnT(old + 2 + k // 2)
                    if k in (5, 7) and core:
                        copy_attnT(g * GROUP + (k - 5) // 2)
                    if core:
                        copy_probsT(g, 2 * k)
                        copy_probsT(g, 2 * k + 1)
                    if k == 1 and prev2:
                        wait(act, s_route, (g - 2) * ROUTE_STEPS + SHIFTED)
                        nc.scalar.activation(prob[:], logits[:], ACT.Exp).then_inc(s_lexp, 1)
                    if k == 3 and nxt:
                        copy_normed(g + 1, 1)
                    if k == 4 and nxt:
                        copy_keys(g + 1)
                    if k == 5 and nxt:
                        copy_queries(g + 1, 1 - u)
                    if k == 7 and prev:
                        wait(act, s_n2T, (g - 1) * 2 + 2)
                        nc.scalar.activation(xn2T[:, 1, :], work[:, 0, :], ACT.Copy).then_inc(s_n2Ta, 1)

            act.wait_ge(s_bias, 64)
            copy_normed(0, 0)
            copy_normed(0, 1)
            copy_keys(0)
            copy_queries(0, 0)
            run_stage_a(act, stage_a)

            def silu(t, u):
                act.wait_ge(s_gate, t + 1)
                nc.scalar.activation(gated[:, u, :], score[:, u, :], ACT.Silu).then_inc(s_silu, 1)

            def copy_fusedT(t, u):
                act.wait_ge(s_ft, t + 1)
                nc.scalar.activation(fusedT[:, u, :], att[:], ACT.Copy).then_inc(s_ftc, 1)

            silu(0, 0)
            def expert_tiles(tt, n):
                for v in range(n):
                    t, u = tt * 4 + v + 1, (1 + v) % 2
                    silu(t, u)
                    copy_fusedT(t - 1, 1 - u)

            with act.Fori(0, STEPS) as tt:
                expert_tiles(tt, 4)
            expert_tiles(STEPS, REST)
            copy_fusedT(TILES - 1, 0)

        @block.vector
        def _(dve):
            def norm_stats(steps, src, eps_out):
                for b in range(GROUP):
                    last = nc.vector.bn_stats(stats[:, b, :], src[:, b, :])
                steps.then(last)
                dve.nop(nofuse=True)
                for b in range(GROUP):
                    last = nc.vector.bn_aggr(mean_var[:, b, :], stats[:, b, :])
                steps.then(last)
                steps.then(nc.vector.tensor_scalar(eps_out[:], mean_var[:, :, 1], EPS, None, ALU.add))

            def normalise(dst, src, scale, signal):
                for b in range(GROUP):
                    last = nc.vector.tensor_scalar(dst[:, b, 0:D], src[:, b, :], mean_var[:, b, 0:1], scale[:, b:b + 1],
                                                   ALU.subtract, ALU.mult)
                last.then_inc(signal, 1)

            def over_experts(col):
                return col.unsqueeze(2).broadcast_to([P, GROUP, EXPERTS])

            def over_group(row):
                return row[:].unsqueeze(1).broadcast_to([P, GROUP, EXPERTS])

            def first_best(steps, values, top, pick, rank):
                steps.then(nc.vector.reduce_max(top[:], values[:], AX.X))
                steps.then(nc.vector.tensor_tensor(tied[:], values[:], over_experts(top[:]), ALU.is_equal))
                steps.then(nc.vector.tensor_tensor(tied[:], tied[:], over_group(first_rank), ALU.mult))
                steps.then(nc.vector.reduce_max(rank, tied[:], AX.X))
                steps.then(nc.vector.tensor_tensor(pick[:], tied[:], over_experts(rank), ALU.is_equal))

            def first_norm_stats(g):
                wait(dve, s_x, g * 16 + 16)
                norm_stats(Steps(dve, s_ln, g * LN_STEPS), x_sb, var_eps)

            def first_norm(g):
                wait(dve, s_rstd, g + 1)
                normalise(xn, x_sb, rstd, s_norm)

            def copy_keys(g):
                wait(dve, s_front, g * 8 + 3)
                wait(dve, s_kb, g * 8)
                nc.vector.tensor_scalar(kT[:, 0, :], work[:, 0, :], bk_sb[:, 0:1], None, ALU.add).then_inc(s_front_v, 1)

            def copy_queries(g, u):
                wait(dve, s_front, g * 8 + 5)
                nc.vector.tensor_scalar(qT[:, u, 0, :], work[:, 0, :], bq_sb[:, 0:1], None, ALU.add).then_inc(s_front_v, 1)

            def copy_values(g, m):
                wait(dve, s_front, g * 8 + 7 + m)
                for s in range(2):
                    last = nc.vector.tensor_tensor(
                        v_aug[:, 2 * m + s, :, 0:DK], work[:, m, s * D:(s + 1) * D].rearrange("p (h r) -> p h r", r=DK),
                        bv_sb[:].rearrange("p (h r) -> p h r", r=DK), ALU.add)
                last.then_inc(s_front_v, 1)

            def shift(g, k):
                c = k % 2
                s = score[:, 2 * c:2 * c + 2, :].rearrange("p q (h t) -> p (q h) t", t=TOK)
                wait(dve, s_score, g * 8 + k + 1)
                nc.vector.reduce_max(row_max[:, c, :], s, AX.X).then_inc(s_max, 1)
                wait(dve, s_max, g * 8 + k + 1)
                wait(dve, s_swap, g * 16 + 2 * k - 2)
                nc.vector.tensor_tensor(probs[:, c], s, row_max[:, c, :].unsqueeze(2).broadcast_to([P, 8, TOK]),
                                        ALU.subtract).then_inc(s_shift, 1)

            def divide_by_sums(i):
                heads = work[:, 0, :].rearrange("p (h r) -> p h r", r=32)
                wait(dve, s_back, i + 1)
                nc.vector.reciprocal(inv_sum[:], heads[:, :, DK]).then_inc(s_inv, 1)
                wait(dve, s_inv, i + 1)
                nc.vector.tensor_tensor(attn[:].rearrange("p (h r) -> p h r", r=DK), heads[:, :, 0:DK],
                                        inv_sum[:].unsqueeze(2).broadcast_to([P, HEADS, DK]), ALU.mult).then_inc(s_attn, 1)

            def add_residual(i, b, u):
                wait(dve, s_proj, i + 1)
                nc.vector.tensor_tensor(x1[:, b, :], work[:, 1, 0:D], x_bo[:, u, b, :], ALU.add).then_inc(s_x1, 1)

            def route_shift(g):
                steps = Steps(dve, s_route, g * ROUTE_STEPS, LN_STEPS)
                wait(dve, s_logit, g + 1)
                raw = work[:, 0, 0:GROUP * 32].rearrange("p (s e) -> p s e", e=32)[:, :, 0:EXPERTS]
                steps.then(nc.vector.reduce_max(best[:], raw, AX.X))
                steps.done(nc.vector.tensor_tensor(logits[:], raw, over_experts(best[:]), ALU.subtract))
                assert steps.n == SHIFTED

            def route_choose(g):
                steps = Steps(dve, s_route, g * ROUTE_STEPS, SHIFTED)
                wait(dve, s_lexp, g + 1)
                steps.then(nc.vector.reduce_sum(total[:], prob[:], AX.X))
                steps.then(nc.vector.reciprocal(share[:], total[:]))
                steps.then(nc.vector.tensor_tensor(prob[:], prob[:], over_experts(share[:]), ALU.mult))
                first_best(steps, prob, top1, pick1, xn2[:, :, RANKS])
                return steps

            def route_choose_second(steps):
                steps.then(nc.vector.scalar_tensor_tensor(rest[:], pick1[:], -2.0, prob[:], ALU.mult, ALU.add))
                first_best(steps, rest, top2, pick2, xn2[:, :, RANKS + 1])
                steps.done(nc.vector.tensor_tensor(gap[:], top2[:], top1[:], ALU.subtract))
                assert steps.n == GAP
                return steps

            def route_count(g, steps):
                steps.done(nc.vector.tensor_tensor(chosen[:], pick1[:], pick2[:], ALU.add))
                steps.then(nc.vector.tensor_tensor(chosen_f[:], pick1[:], pick2[:], ALU.add))
                for b in range(GROUP):
                    steps.then(nc.vector.tensor_tensor(seen[:, b + 1, :], seen[:, b, :], chosen_f[:, b, :], ALU.add))
                steps.then(nc.vector.tensor_copy(seen_bf[:], seen[:]))
                assert steps.n == CHOSEN
                steps.done(nc.vector.tensor_copy(seen[:, 0, :], seen[:, GROUP, :]))
                return steps

            def route_weights(g, steps):
                wait(dve, s_gexp, g + 1)
                w1, w2 = (xn2[:, :, WEIGHTS + k] for k in range(2))
                steps.then(nc.vector.tensor_scalar(total[:], gap[:], 1.0, None, ALU.add))
                steps.then(nc.vector.reciprocal(w1, total[:]))
                steps.done(nc.vector.tensor_tensor(w2, gap[:], w1, ALU.mult))
                steps.done(nc.vector.tensor_scalar(xn2[:, :, TOKEN], xn2[:, :, TOKEN], float(GROUP * TOK), None, ALU.add))
                return steps

            def route_read_places(g, steps):
                wait(dve, s_place, g + 1)
                steps.then(nc.vector.tensor_tensor(place[:], work[:, 1, 0:GROUP * EXPERTS].rearrange("p (s e) -> p s e", e=EXPERTS),
                                                   over_group(region_base), ALU.add))
                assert steps.n == PLACES_READ, steps.n
                return steps

            def route_place(g, steps):
                steps.wait()
                for k, pick in enumerate((pick1, pick2)):
                    steps.then(nc.vector.tensor_tensor(picked[:], pick[:], place[:], ALU.mult))
                    steps.then(nc.vector.reduce_sum(slot_f[:, k * GROUP:(k + 1) * GROUP], picked[:], AX.X))
                if not isinstance(g, int) or g > 0:
                    wait(dve, s_scat, BLANKS * 16 + g * 2 * GROUP * 16)
                steps.done(nc.vector.tensor_copy(slots_now[:], slot_f[:]))
                assert steps.n == ROUTE_STEPS, steps.n

            rounds = iter([0, 1, 0, 1, 0, 1, 0, 1])

            def stage_a(g, core, prev, prev2, nxt, far):
                u = next(rounds)
                old = (g - 1) * GROUP
                for k in range(8):
                    if core and k != 3:
                        shift(g, k)
                    if k == 0:
                        if prev:
                            add_residual(old + 1, 1, 1 - u)
                            divide_by_sums(old + 2)
                        if nxt:
                            first_norm_stats(g + 1)
                        if core:
                            copy_values(g, 0)
                    if k == 1:
                        if core:
                            copy_values(g, 1)
                        if nxt:
                            first_norm(g + 1)
                    if k == 2:
                        if prev2:
                            route_shift(g - 2)
                        if core:
                            shift(g, 3)
                        if prev:
                            add_residual(old + 2, 2, 1 - u)
                            divide_by_sums(old + 3)
                        if prev2:
                            routing = route_choose(g - 2)
                    if k == 3:
                        if prev2:
                            routing = route_choose_second(routing)
                            routing = route_count(g - 2, routing)
                    if k == 4:
                        if prev:
                            add_residual(old + 3, 3, 1 - u)
                        if core:
                            divide_by_sums(g * GROUP)
                        if prev2:
                            routing = route_weights(g - 2, routing)
                            routing = route_read_places(g - 2, routing)
                            route_place(g - 2, routing)
                        if nxt:
                            copy_keys(g + 1)
                    if k == 5:
                        if nxt:
                            copy_queries(g + 1, 1 - u)
                        if prev:
                            wait(dve, s_x1, g * GROUP)
                            norm_stats(Steps(dve, s_route, (g - 1) * ROUTE_STEPS), x1, var_eps2)
                    if k == 6:
                        if prev:
                            wait(dve, s_rstd2, g)
                            wait(dve, s_scat, BLANKS * 16 + (g - 1) * 2 * GROUP * 16)
                            normalise(xn2, x1, rstd2, s_norm2)
                        if core:
                            if prev:
                                wait(dve, s_res, g * 16)
                                wait(dve, s_norm2, g)
                            add_residual(g * GROUP, 0, u)
                            divide_by_sums(g * GROUP + 1)
                    if k == 7 and prev:
                        wait(dve, s_n2T, (g - 1) * 2 + 1)
                        nc.vector.tensor_copy(xn2T[:, 0, :], work[:, 0, :]).then_inc(s_n2Tv, 1)

            dve.wait_ge(s_bias, 64)
            dve.wait_ge(s_const, 11)
            dve.wait_ge(s_masks, 5)
            first_norm_stats(0)
            first_norm(0)
            copy_keys(0)
            copy_queries(0, 0)
            run_stage_a(dve, stage_a)

            steps = Steps(dve, s_table)
            dve.wait_ge(s_count, 1)
            steps.then(nc.vector.tensor_tensor(count[:], work[:, 0, 0:EXPERTS], blank[:, 0:EXPERTS], ALU.add))
            steps.then(nc.vector.scalar_tensor_tensor(pad_f[:], count[:], lane[:, 0:1], region_base[:], ALU.add, ALU.add))
            steps.then(nc.vector.tensor_copy(pad_rows[:], pad_f[:]))
            assert steps.n == PADS_MADE
            m = TOKENS // P
            dve.wait_ge(s_const, 12)
            steps.then(nc.vector.tensor_tensor(over, count[:].unsqueeze(2).broadcast_to([P, EXPERTS, m]), edges, ALU.is_gt))
            steps.then(nc.vector.reduce_sum(n_tiles[:], over, AX.X))
            steps.then(nc.vector.tensor_copy(tiles_to[:], n_tiles[:]))
            for e in range(1, EXPERTS):
                steps.then(nc.vector.tensor_tensor(tiles_to[:, e:e + 1], tiles_to[:, e - 1:e], n_tiles[:, e:e + 1], ALU.add))
            by_expert = [P, TABLE, EXPERTS]
            steps.then(nc.vector.tensor_tensor(past, tiles_to[:].unsqueeze(1).broadcast_to(by_expert),
                                               tile_no[:].unsqueeze(2).broadcast_to(by_expert), ALU.is_le))
            steps.then(nc.vector.reduce_sum(expert_f[:], past, AX.X))
            steps.then(nc.vector.tensor_tensor(past_tiles, past, n_tiles[:].unsqueeze(1).broadcast_to(by_expert), ALU.mult))
            steps.then(nc.vector.reduce_sum(skipped[:], past_tiles, AX.X))
            steps.then(nc.vector.tensor_tensor(row_f[:], tile_no[:], skipped[:], ALU.subtract))
            steps.then(nc.vector.tensor_scalar(skipped[:], expert_f[:], float(REGION), None, ALU.mult))
            steps.then(nc.vector.scalar_tensor_tensor(row_f[:], row_f[:], float(P), skipped[:], ALU.mult, ALU.add))
            steps.then(nc.vector.tensor_copy(row_table[:], row_f[0:1]))
            steps.then(nc.vector.tensor_scalar(expert_f[:], expert_f[:], float(EXPERTS - 1), None, ALU.min))
            steps.then(nc.vector.tensor_copy(expert_table[:], expert_f[0:1]))
            steps.then(nc.vector.tensor_scalar(tile_rank[:], expert_f[:], -1.0, float(EXPERTS), ALU.mult, ALU.add))
            assert steps.n == TABLE_STEPS, steps.n

            def copy_tileT(t, u):
                dve.wait_ge(s_xt, t + 1)
                nc.vector.tensor_copy(xsT[:, u, :], swap[:, 0:DC * P]).then_inc(s_xtc, 1)

            def fuse(t, u):
                dve.wait_ge(s_silu, t + 1)
                dve.wait_ge(s_up, t + 1)
                nc.vector.tensor_tensor(fused[:, u, :], gated[:, u, :], score[:, 2 + u, :], ALU.mult).then_inc(s_fuse, 1)

            def read_rows_ends(t, u, v, loads):
                dve.wait_ge(s_xs[u], loads * 16)
                nc.vector.scalar_tensor_tensor(pair[:], xs[:, u, RANKS:RANKS + 2], tile_rank[:, bass.ds(t, 1)],
                                               xs[:, u, WEIGHTS:WEIGHTS + 2], ALU.is_equal, ALU.mult).then_inc(s_pair, 1)
                nc.vector.tensor_copy(token[:, v, :], xs[:, u, TOKEN:ROW])
                dve.wait_ge(s_pair, t + 1)
                nc.vector.reduce_sum(weight[:, v, :], pair[:], AX.X).then_inc(s_meta, 1)

            def copy_y(t, u, v):
                dve.wait_ge(s_down, t + 1)
                nc.vector.tensor_scalar(ys[:, u, :], work[:, u, 0:D], weight[:, v, :], None, ALU.mult).then_inc(s_y, 1)

            copy_tileT(0, 0)
            read_rows_ends(0, 0, 0, 1)
            copy_tileT(1, 1)
            dve.wait_ge(s_meta, 1)
            read_rows_ends(1, 1, 1, 1)
            fuse(0, 0)

            def expert_tiles(tt, first, n):
                for v in range(n):
                    t, u = tt * 4 + v + 1, (1 + v) % 2
                    fuse(t, u)
                    copy_tileT(t + 1, 1 - u)
                    dve.wait_ge(s_meta, t + 1)
                    if not first or v > 1:
                        dve.wait_ge(s_acc, (t - 2) * 16)
                    read_rows_ends(t + 1, 1 - u, (v + 2) % 4, tt * 2 + v // 2 + 2)
                    copy_y(t - 1, 1 - u, v)

            expert_tiles(0, True, 4)
            with dve.Fori(1, STEPS) as tt:
                expert_tiles(tt, False, 4)
            expert_tiles(STEPS, False, REST)
            dve.wait_ge(s_acc, (TILES - 2) * 16)
            copy_y(TILES - 1, 0, (TILES - 1) % 4)


_INS = ['x', 'ctx_1024', 'L0_xattn_Wq', 'L0_xattn_bq', 'L0_xattn_Wk', 'L0_xattn_bk', 'L0_xattn_Wv', 'L0_xattn_bv',
        'L0_xattn_Wo', 'L0_xattn_bo', 'L0_ffn_kernel_router_DE', 'L0_ffn_kernel_gating_EDF',
        'L0_ffn_kernel_up_EDF', 'L0_ffn_kernel_down_EFD']


def kernel(**inputs):
    import numpy as _np
    import concourse.bacc as _bacc
    from concourse.bass_utils import run_bass_kernel_spmd as _run

    nc = _bacc.Bacc("TRN2", target_bir_lowering=False, num_devices=1)
    arrays, args = {}, []
    for name in _INS:
        a = _np.asarray(inputs[name])
        if name == 'ctx_1024':
            a = a.reshape(TOKENS, D).T
        a = _np.ascontiguousarray(a)
        arrays[f"in_{name}"] = a
        args.append(nc.dram_tensor(f"in_{name}", a.shape, mybir.dt.from_np(a.dtype), kind="ExternalInput").ap())
    out = nc.dram_tensor("out_0", (TOKENS + P, D), mybir.dt.float32, kind="ExternalOutput").ap()
    moe_attention(nc, *args, out)
    r = _run(nc, [arrays], core_ids=[0])
    return r.results[0]["out_0"][:TOKENS].reshape(SEQS, TOK, D)
```
